# Optimizing a Trainium2 kernel written in Bass

```python
import numpy as np
import jax
import jax.numpy as jnp

def _softmax(x, axis=-1):
    return jax.nn.softmax(x, axis=axis)

def _gelu(x):
    return jax.nn.gelu(x, approximate=True)

def _silu(x):
    return jax.nn.silu(x)

def _sigmoid(x):
    return jax.nn.sigmoid(x)

def _layernorm(x, axis=-1, eps=1e-05):
    m = jnp.mean(x, axis=axis, keepdims=True)
    v = jnp.var(x, axis=axis, keepdims=True)
    return (x - m) / jnp.sqrt(v + eps)

def _scatter_add(tgt, idx, src, axis=0):
    return tgt.at[idx].add(src)

def _segment_sum(src, seg, n):
    return jax.ops.segment_sum(src, seg, n)
kernel_name = 'mk_flamingo_gated_d1_seqx_r2_8a8de3'

def setup_inputs(seed: int=0):
    np.random.seed(seed)
    _w = jnp.asarray

    def _rec_inputs():
        import jax
        import jax.numpy as jnp
        _rk = jax.random.key(seed)
        x = -0.0003929 + 0.9999 * jax.random.normal(jax.random.fold_in(_rk, 1), (8, 224, 2048), jnp.float32)
        _lenS = 224 - jax.random.randint(jax.random.fold_in(_rk, 7), (8,), 0, max(1, 224 // 4) + 1, jnp.int32)
        _lenS2 = 750 - jax.random.randint(jax.random.fold_in(_rk, 8), (8,), 0, max(1, 750 // 4) + 1, jnp.int32)
        _ctx_1024P = jax.random.normal(jax.random.fold_in(_rk, 11), (8, 16, 512), jnp.float32)
        _ctx_1024c = jax.random.dirichlet(jax.random.fold_in(_rk, 511), 0.3 * jnp.ones((16,), jnp.float32), (8, 750))
        _ctx_1024t = jnp.einsum('bsk,bkd->bsd', _ctx_1024c, _ctx_1024P)
        _ctx_1024t = _ctx_1024t * jax.lax.rsqrt(jnp.mean(jnp.square(_ctx_1024t)) + 1e-12) * 0.953939
        ctx_1024 = -1.39393e-06 + 0.999914 * (_ctx_1024t + 0.3 * jax.random.normal(jax.random.fold_in(_rk, 611), (8, 750, 512), jnp.float32))
        _validS = jnp.arange(224)[None, :] < _lenS[:, None]
        _validS2 = jnp.arange(750)[None, :] < _lenS2[:, None]
        _causal = jnp.tril(jnp.ones((224, 224), dtype=bool))
        mask_SxS2_ff0 = jnp.where(jnp.ones((224, 750), dtype=bool), 0.0, -1000000000.0).astype(jnp.float32)
        _g = jax.random.normal(jax.random.fold_in(_rk, 9001), (2, 1), jnp.float32)
        _g = jnp.sign(_g) * jnp.maximum(jnp.abs(_g), 1.0) + (_g == 0) * 1.0
        g_xattn = _g[0]
        g_ffn = _g[1]
        return (x, ctx_1024, mask_SxS2_ff0, g_xattn, g_ffn)
    x, ctx_1024, mask_SxS2_ff0, g_xattn, g_ffn = _rec_inputs()

    def _L0_xattn_setup():
        import math
        import jax, jax.numpy as jnp
        import numpy as np
        N_HEADS = 32
        N_KV_HEADS = 8
        N_REP = N_HEADS // N_KV_HEADS
        HEAD_DIM = 2048 // N_HEADS
        key = jax.random.key(seed)
        kq, kk, kv = jax.random.split(key, 3)
        B, S, T = (2, 1024, 1024)
        q = jax.random.normal(kq, (B, S, N_HEADS * HEAD_DIM), dtype=jnp.float32)
        k = jax.random.normal(kk, (B, T, N_KV_HEADS * HEAD_DIM), dtype=jnp.float32)
        v = jax.random.normal(kv, (B, T, N_KV_HEADS * HEAD_DIM), dtype=jnp.float32)
        mask = jnp.zeros((S, T), dtype=jnp.float32)
        return {'q': q, 'k': k, 'v': v, 'start_pos': 0, 'mask': mask}
    _L0_xattn_all = _L0_xattn_setup()
    _L0_xattn_in = {k: v for k, v in _L0_xattn_all.items() if k in ()}
    del _L0_xattn_all

    def _L0_ffn_setup():
        import jax, jax.numpy as jnp
        import numpy as np
        HID, BOT, RDIM, NSLOT, K, VB = (2048, 64, 48, 512, 8, 128)
        TAU_LOW, TAU_HIGH, EARLY_EXIT = (0.5, 2.0, 0.05)

        def _uncertainty(h, Wu1, bu1, Wu2, bu2):
            var = jnp.var(h, axis=-1)
            log_var = jnp.log1p(var)
            norm_var = log_var / (jnp.mean(log_var) + 1e-06)
            learned = (jax.nn.gelu(h @ Wu1.T + bu1) @ Wu2.T + bu2)[..., 0]
            return jnp.clip(norm_var * 0.5 + jax.nn.sigmoid(learned) * 2.5, 0.0, 5.0)
        key = jax.random.key(seed)
        ks = jax.random.split(key, 12)
        B, S = (2, 1024)
        return {'hidden_states': jax.random.normal(ks[0], (B, S, HID), dtype=jnp.float32), 'Wq': jax.random.normal(ks[1], (BOT, HID), dtype=jnp.float32) / np.sqrt(HID), 'Wr': jax.random.normal(ks[2], (RDIM, BOT), dtype=jnp.float32) / np.sqrt(BOT), 'aux_keys': jax.random.normal(ks[3], (NSLOT, BOT), dtype=jnp.float32) * 0.01, 'aux_values': jax.random.normal(ks[4], (NSLOT, HID), dtype=jnp.float32) * 0.02, 'Wvd': jax.random.normal(ks[5], (VB, HID), dtype=jnp.float32) * 0.1 / np.sqrt(HID), 'Wvu': jax.random.normal(ks[6], (HID, VB), dtype=jnp.float32) * 0.1 / np.sqrt(VB), 'Wu1': jax.random.normal(ks[7], (HID // 4, HID), dtype=jnp.float32) / np.sqrt(HID), 'bu1': jnp.zeros((HID // 4,), dtype=jnp.float32), 'Wu2': jax.random.normal(ks[8], (1, HID // 4), dtype=jnp.float32) * 0.01, 'bu2': jnp.zeros((1,), dtype=jnp.float32), 'gate_w1': jnp.float32(0.5), 'gate_bias': jnp.float32(-1.0), 'log_rel': jnp.zeros((NSLOT,), dtype=jnp.float32)}
    _L0_ffn_all = _L0_ffn_setup()
    _L0_ffn_in = {k: v for k, v in _L0_ffn_all.items() if k in ('Wq', 'Wr', 'aux_keys', 'aux_values', 'Wvd', 'Wvu', 'Wu1', 'bu1', 'Wu2', 'bu2', 'gate_w1', 'gate_bias', 'log_rel')}
    del _L0_ffn_all
    return {'x': x, 'ctx_1024': ctx_1024, 'mask_SxS2_ff0': mask_SxS2_ff0, 'g_xattn': g_xattn, 'g_ffn': g_ffn, 'L0_ffn_Wq': _L0_ffn_in['Wq'], 'L0_ffn_Wr': _L0_ffn_in['Wr'], 'L0_ffn_aux_keys': _L0_ffn_in['aux_keys'], 'L0_ffn_aux_values': _L0_ffn_in['aux_values'], 'L0_ffn_Wvd': _L0_ffn_in['Wvd'], 'L0_ffn_Wvu': _L0_ffn_in['Wvu'], 'L0_ffn_Wu1': _L0_ffn_in['Wu1'], 'L0_ffn_bu1': _L0_ffn_in['bu1'], 'L0_ffn_Wu2': _L0_ffn_in['Wu2'], 'L0_ffn_bu2': _L0_ffn_in['bu2'], 'L0_ffn_gate_w1': _L0_ffn_in['gate_w1'], 'L0_ffn_gate_bias': _L0_ffn_in['gate_bias'], 'L0_ffn_log_rel': _L0_ffn_in['log_rel']}

def reference(x, ctx_1024, mask_SxS2_ff0, g_xattn, g_ffn, L0_ffn_Wq, L0_ffn_Wr, L0_ffn_aux_keys, L0_ffn_aux_values, L0_ffn_Wvd, L0_ffn_Wvu, L0_ffn_Wu1, L0_ffn_bu1, L0_ffn_Wu2, L0_ffn_bu2, L0_ffn_gate_w1, L0_ffn_gate_bias, L0_ffn_log_rel):
    import jax
    import jax.numpy as jnp

    def _L0_xattn_ref(q, k, v, start_pos, mask):
        import math
        import jax, jax.numpy as jnp
        import numpy as np
        N_HEADS = 32
        N_KV_HEADS = 8
        N_REP = N_HEADS // N_KV_HEADS
        HEAD_DIM = 2048 // N_HEADS
        b, s, _ = q.shape
        t = k.shape[1]
        xq = q.reshape(b, s, N_KV_HEADS, N_REP, HEAD_DIM)
        xk = k.reshape(b, t, N_KV_HEADS, HEAD_DIM)
        xv = v.reshape(b, t, N_KV_HEADS, HEAD_DIM)
        scores = jnp.einsum('bsgrd,btgd->bgrst', xq, xk) / math.sqrt(HEAD_DIM)
        scores = scores + mask
        probs = jax.nn.softmax(scores.astype(jnp.float32), axis=-1).astype(q.dtype)
        out = jnp.einsum('bgrst,btgd->bsgrd', probs, xv)
        return out.reshape(b, s, N_HEADS * HEAD_DIM)

    def _L0_ffn_ref(hidden_states, Wq, Wr, aux_keys, aux_values, Wvd, Wvu, Wu1, bu1, Wu2, bu2, gate_w1, gate_bias, log_rel):
        import jax, jax.numpy as jnp
        import numpy as np
        HID, BOT, RDIM, NSLOT, K, VB = (2048, 64, 48, 512, 8, 128)
        TAU_LOW, TAU_HIGH, EARLY_EXIT = (0.5, 2.0, 0.05)

        def _uncertainty(h, Wu1, bu1, Wu2, bu2):
            var = jnp.var(h, axis=-1)
            log_var = jnp.log1p(var)
            norm_var = log_var / (jnp.mean(log_var) + 1e-06)
            learned = (jax.nn.gelu(h @ Wu1.T + bu1) @ Wu2.T + bu2)[..., 0]
            return jnp.clip(norm_var * 0.5 + jax.nn.sigmoid(learned) * 2.5, 0.0, 5.0)
        query = hidden_states @ Wq.T
        rq = query @ Wr.T
        rk = aux_keys @ Wr.T
        router_scores = jnp.einsum('bsr,nr->bsn', rq, rk) / np.sqrt(RDIM) + log_rel
        top_scores, top_idx = jax.lax.top_k(router_scores, K)
        sel_keys = aux_keys[top_idx]
        attn = jnp.einsum('bsd,bskd->bsk', query, sel_keys) / np.sqrt(BOT) + log_rel[top_idx]
        w = jax.nn.softmax(attn, axis=-1)
        sel_vals = aux_values[top_idx]
        aux_out = jnp.einsum('bsk,bskh->bsh', w, sel_vals)
        aux_out = aux_out @ Wvd.T @ Wvu.T
        u = _uncertainty(hidden_states, Wu1, bu1, Wu2, bu2)
        u_norm = jnp.clip((u - TAU_LOW) / (TAU_HIGH - TAU_LOW), 0.0, 1.0)
        gate = jax.nn.sigmoid(gate_w1 * u_norm + gate_bias)
        gate = jnp.where(gate < EARLY_EXIT, 0.0, gate)
        return hidden_states + gate[..., None] * aux_out
    x = x + jnp.tanh(g_xattn[0]) * _L0_xattn_ref(_layernorm(x, axis=-1), ctx_1024, ctx_1024, 0, mask_SxS2_ff0)
    x = x + jnp.tanh(g_ffn[0]) * _L0_ffn_ref(_layernorm(x, axis=-1), L0_ffn_Wq, L0_ffn_Wr, L0_ffn_aux_keys, L0_ffn_aux_values, L0_ffn_Wvd, L0_ffn_Wvu, L0_ffn_Wu1, L0_ffn_bu1, L0_ffn_Wu2, L0_ffn_bu2, L0_ffn_gate_w1, L0_ffn_gate_bias, L0_ffn_log_rel)
    return x

_drawn_inputs = setup_inputs


def setup_inputs(seed=0):
    import zlib

    import numpy as np

    out = dict(_drawn_inputs(seed))
    spreads = {'mask_SxS2_ff0': (0.0, 0.8), 'L0_ffn_bu1': (0.0, 0.8), 'L0_ffn_log_rel': (0.0, 0.8)}
    factors = {'L0_ffn_Wq': 8.0,
     'L0_ffn_Wr': 8.0,
     'L0_ffn_aux_keys': 8.0,
     'L0_ffn_aux_values': 8.0,
     'L0_ffn_Wvd': 8.0,
     'L0_ffn_Wvu': 8.0,
     'L0_ffn_Wu1': 8.0,
     'L0_ffn_Wu2': 8.0}
    for name, (base, spread) in spreads.items():
        noise = np.random.default_rng([zlib.crc32(name.encode()), seed]).standard_normal(out[name].shape)
        drawn = base * np.exp(spread * noise) if base else spread * noise
        out[name] = jnp.asarray(drawn.astype(out[name].dtype))
    for name, factor in factors.items():
        out[name] = (out[name] * factor).astype(out[name].dtype)
    return out
```

```python
from contextlib import ExitStack

import concourse.bass as bass
from concourse import mybir

ALU = mybir.AluOpType
ACT = mybir.ActivationFunctionType
AX = mybir.AxisListType
F32 = mybir.dt.float32
BF16 = mybir.dt.bfloat16

BATCH, SEQ, HID = 8, 224, 2048
CTX, CDIM = 750, 512
HEADS, KV = 32, 8
REP = HEADS // KV
D = HID // HEADS
HALF = SEQ // 2
NCH = 6
TC = CTX // NCH
GROUPS = BATCH * KV
NHALF = 2 * GROUPS
TILES = NHALF * REP
PAIRS = GROUPS // 2
PER_PAIR = 2 * 2 * REP
GW = REP * D
EPS = 1e-5
BOT, RDIM, NSLOT, TOPK, VB, F1 = 64, 48, 512, 8, 128, HID // 4
KC = HID // 128
FFN_TILES = 2 * BATCH
ROWS = BATCH * SEQ
TAU_LOW, TAU_HIGH, EARLY_EXIT = 0.5, 2.0, 0.05
ARENA = 19152
GATE_EXP = 11
GATE_BASE = 19


def high(ap):
    return ap.bitcast(BF16)[..., 1::2]


def flamingo_block(nc, x, k_t, v_rows, mask, g_x, av_t, wvd_t, w1_t, wq_t, wr, keys_t, log_rel, b1, w2, wvu_t, scalars, out):
    with ExitStack() as ctx:
        def sb(name, shape, dt=F32):
            return ctx.enter_context(nc.sbuf_tensor(name, shape, dt))

        def pb(name, shape):
            return ctx.enter_context(nc.psum_tensor(name, shape, F32))

        def sem(name):
            return ctx.enter_context(nc.semaphore(name))

        x_sb = sb("x_sb", [HALF, GROUPS * 2 * GW])
        x5 = x_sb[:, :].rearrange("p (b g h c) -> p b g h c", b=BATCH, g=KV, h=2)
        ident = sb("ident", [128, 128])
        tanh_gx = sb("tanh_gx", [HALF, 1])
        stats = sb("stats", [HALF, 2, KV, 6])
        meanvar = sb("meanvar", [HALF, 16, 2])
        veps = sb("veps", [HALF, 16])
        minus_half = sb("minus_half", [HALF, 16])
        rstd = sb("rstd", [HALF, 16])
        ln_mean = sb("ln_mean", [HALF, PAIRS, 2])
        ln_scale = sb("ln_scale", [HALF, PAIRS, 2])

        arena = sb("arena", [128, ARENA])
        used = {"attention": 0, "ffn": 0}

        def carve(phase, shape, dt=F32):
            words = 1
            for n in shape[1:]:
                words *= n
            words = words * (2 if dt == BF16 else 4) // 4
            at = used[phase]
            used[phase] = at + words
            assert used[phase] <= ARENA, (phase, used[phase])
            ap = arena[0:shape[0], at:at + words]
            ap = ap.bitcast(BF16) if dt == BF16 else ap
            if len(shape) == 3:
                ap = ap.rearrange("p (a b) -> p a b", a=shape[1])
            elif len(shape) == 4:
                ap = ap.rearrange("p (a b c) -> p a b c", a=shape[1], b=shape[2])
            elif len(shape) == 5:
                ap = ap.rearrange("p (a b c d) -> p a b c d", a=shape[1], b=shape[2], c=shape[3])
            return ap

        mask_sb = carve("attention", [HALF, 2, CTX])
        k_raw = carve("attention", [128, 2, CTX])
        k_hi = carve("attention", [128, 2, CTX], BF16)
        k_lo = carve("attention", [128, 2, CTX], BF16)
        v_raw = carve("attention", [TC, 2, NCH, D])
        v_hi = carve("attention", [TC, 2, NCH, D + 1], BF16)
        v_lo = carve("attention", [TC, 2, NCH, D], BF16)
        q_rows = carve("attention", [HALF, 2, REP, 2, D])
        q_t = carve("attention", [128, 2, REP * HALF], BF16)
        s_sb = carve("attention", [HALF, 4, CTX])
        row_max = carve("attention", [HALF, 4, 1])
        p_sb = carve("attention", [TC, 4, NCH * HALF])
        p_lo = carve("attention", [TC, 4, NCH * HALF], BF16)
        r_den = carve("attention", [HALF, 2, REP])

        w1_hi = carve("ffn", [128, KC, F1], BF16)
        w1_lo = carve("ffn", [128, KC, F1], BF16)
        wq_cat = carve("ffn", [128, KC, 2 * BOT], BF16)
        h_rows = carve("ffn", [HALF, 2, 4 * GW])
        h_hi = carve("ffn", [128, 4, 4, HALF], BF16)
        h_lo = carve("ffn", [128, 4, 4, HALF], BF16)
        keys_aug = carve("ffn", [128, NSLOT])
        rk_aug = carve("ffn", [128, NSLOT])
        v2 = carve("ffn", [128, 4, VB])
        z_all = carve("ffn", [128, 2 * BATCH * HALF])
        q_aug = carve("ffn", [128, HALF])
        rq_aug = carve("ffn", [128, HALF])
        q_tmp = carve("ffn", [64, HALF])
        gelu_t = carve("ffn", [128, 4, HALF])
        w_rows = carve("ffn", [HALF, NSLOT])
        w_t = carve("ffn", [128, 4, HALF])
        rest = carve("ffn", [HALF, NSLOT])
        unsel = carve("ffn", [HALF, NSLOT])
        wvu = arena[:, 0:HID]
        z_cur = arena[:, HID:HID + 2 * HALF].rearrange("p (h c) -> p h c", h=2)

        stage_at = ARENA - 4560
        assert used["attention"] <= stage_at
        stage = arena[:, stage_at:stage_at + 2 * 4 * F1].rearrange("p (s k n) -> p s k n", s=2, k=4)
        wq_raw = arena[:, 9216:9216 + KC * BOT].rearrange("p (k n) -> p k n", k=KC)
        wvd_sb = arena[:, 6144:6144 + KC * VB].rearrange("p (k n) -> p k n", k=KC)
        wr_t = sb("wr_t", [128, RDIM])
        bu1 = sb("bu1", [128, 4])
        wu2 = sb("wu2", [128, 4])
        scal = sb("scal", [HALF, 4])
        tanh_gf = sb("tanh_gf", [HALF, 1])
        ones = sb("ones", [HALF, HALF])
        bn2 = sb("bn2", [HALF, 4, 6])
        mv2 = sb("mv2", [HALF, 2])
        ve2 = sb("ve2", [HALF, 1])
        half2 = sb("half2", [HALF, 1])
        rs2 = sb("rs2", [HALF, 1])
        top8 = sb("top8", [HALF, 8])
        neg_top = sb("neg_top", [HALF, 1])
        w_sum = sb("w_sum", [HALF, 1])
        mean_all = sb("mean_all", [HALF, FFN_TILES])
        var_all = sb("var_all", [HALF, FFN_TILES])
        rstd_all = sb("rstd_all", [HALF, FFN_TILES])
        wsum_all = sb("wsum_all", [HALF, FFN_TILES])
        learned = sb("learned", [HALF, FFN_TILES])
        gate = sb("gate", [HALF, 12, FFN_TILES])

        psum = pb("psum", [128, 8, 512])
        score_ps = psum[:, 0:4, :].rearrange("p (s c) n -> p s c n", s=2)
        tr_ps = psum[:, 4:6, :]
        mix_ps = psum[:, 6:8, :]

        s_const = sem("s_const")
        s_ident = sem("s_ident")
        s_init = sem("s_init")
        s_gx = sem("s_gx")
        s_tanh = sem("s_tanh")
        x_loaded = [sem(f"x_loaded{b}") for b in range(BATCH)]
        s_mask = sem("s_mask")
        s_bn = sem("s_bn")
        s_agg = sem("s_agg")
        s_rstd = sem("s_rstd")
        s_veps = sem("s_veps")
        s_ln = sem("s_ln")
        k_loaded = [sem("k_loaded0"), sem("k_loaded1")]
        v_loaded = [sem("v_loaded0"), sem("v_loaded1")]
        k_hi_done = sem("k_hi_done")
        k_split = sem("k_split")
        v_hi_done = sem("v_hi_done")
        v_split = sem("v_split")
        q_staged = sem("q_staged")
        q_turned = sem("q_turned")
        q_hi_done = sem("q_hi_done")
        q_split = sem("q_split")
        scored = sem("scored")
        passed = sem("passed")
        maxed = sem("maxed")
        shifted_v = sem("shifted_v")
        shifted_a = sem("shifted_a")
        turned = sem("turned")
        exped = sem("exped")
        p_split = sem("p_split")
        mixed = sem("mixed")
        den_done = sem("den_done")
        x_added = sem("x_added")
        s_out = sem("s_out")

        stage_loaded = [sem("stage_loaded0"), sem("stage_loaded1")]
        weights_loaded = sem("weights_loaded")
        small_loaded = sem("small_loaded")
        pads_set = sem("pads_set")
        v2_piece = sem("v2_piece")
        w1_hi_done = sem("w1_hi_done")
        w1_split = sem("w1_split")
        wq_hi_done = sem("wq_hi_done")
        wq_split = sem("wq_split")
        rk_summed = sem("rk_summed")
        tables_ready = sem("tables_ready")
        bn2_done = sem("bn2_done")
        mv2_done = sem("mv2_done")
        ve2_done = sem("ve2_done")
        rs2_done = sem("rs2_done")
        logits_done = sem("logits_done")
        sq_done = sem("sq_done")
        h_staged = sem("h_staged")
        h_turned = sem("h_turned")
        h_hi_done = sem("h_hi_done")
        h_split = sem("h_split")
        quad_used = sem("quad_used")
        q_half = sem("q_half")
        q_ready = sem("q_ready")
        rq_summed = sem("rq_summed")
        rq_ready = sem("rq_ready")
        routed = sem("routed")
        topped = sem("topped")
        selected = sem("selected")
        weighed = sem("weighed")
        w_turned = sem("w_turned")
        w_t_ready = sem("w_t_ready")
        z_summed = sem("z_summed")
        z_ready = sem("z_ready")
        gelu_done = sem("gelu_done")
        learned_summed = sem("learned_summed")
        learned_kept = sem("learned_kept")
        ones_set = sem("ones_set")
        wvu_loaded = sem("wvu_loaded")
        gf_tanh = sem("gf_tanh")
        log_var_done = sem("log_var_done")
        mean_summed = sem("mean_summed")
        gate_v = sem("gate_v")
        gate_a = sem("gate_a")
        z_copied = sem("z_copied")
        aux_summed = sem("aux_summed")
        base_done = sem("base_done")
        y_done = sem("y_done")

        block = ctx.enter_context(nc.Block())

        def shifts_on_act(k):
            return k % 2 == 1

        def sweep(eng, step):
            for k in range(-8, 0):
                step(0, k, False)
            with eng.Fori(0, PAIRS - 1) as pair:
                for k in range(PER_PAIR):
                    step(pair, k, False)
            for k in range(PER_PAIR + 2):
                step(PAIRS - 1, k, True)

        def sweep_tiles(eng, step):
            for i in (-1, 0, 1):
                step(0, i)
            with eng.Fori(1, BATCH - 1) as b:
                for i in range(2):
                    step(b, i)
            for i in range(4):
                step(BATCH - 1, i)

        def in_range(b, i):
            return not isinstance(b, int) or 0 <= 2 * b + i < FFN_TILES

        def from_tile(b, i, first):
            return not isinstance(b, int) or 2 * b + i >= first

        def rows_of(b, i):
            flat = x_sb[:, bass.ds(b * (2 * HID) + i // 2 * (2 * HID), 2 * HID)]
            return flat.rearrange("p (g h c) -> p g h c", g=KV, h=2)[:, :, i % 2, :]

        def count(pair, per_pair, local):
            return pair * per_pair + local

        @block.sync
        def _(sp):
            sp.dma_start(x5[:, 0], x[0]).then_inc(x_loaded[0], 16)

            def load(pair, u):
                g = count(pair, 2, u)
                for part in range(2):
                    sp.dma_start(k_raw[D * part:D * part + D, u, :], k_t[bass.ds(g, 1)].rearrange("o d t -> (o d) t")).then_inc(k_loaded[u], 16)
                sp.dma_start(v_raw[:, u], v_rows[bass.ds(g, 1)].rearrange("o p (c d) -> (o p) c d", c=NCH)).then_inc(v_loaded[u], 16)

            load(0, 0)
            load(0, 1)
            for i in range(2):
                sp.dma_start(stage[:, i], av_t[i]).then_inc(stage_loaded[i], 16)
            for dst, src in ((wr_t[0:BOT], wr), (bu1, b1), (wu2, w2), (scal, scalars)):
                sp.dma_start(dst[:], src).then_inc(small_loaded, 16)
            with sp.Fori(1, PAIRS) as pair:
                for u in range(2):
                    sp.wait_ge(k_split, count(pair, 2, u - 1))
                    sp.wait_ge(v_split, count(pair, 2, u - 1))
                    load(pair, u)
            sp.wait_ge(x_added, NHALF)
            sp.dma_start(wvd_sb, wvd_t).then_inc(weights_loaded, 16)
            sp.dma_start(keys_aug[0:BOT, :], keys_t).then_inc(weights_loaded, 16)
            sp.dma_start(wq_raw, wq_t).then_inc(weights_loaded, 16)
            for i in range(2, 8):
                if i - 2 < 4:
                    sp.wait_ge(v2_piece, i - 1)
                else:
                    sp.wait_ge(w1_split, i - 5)
                src = av_t[i] if i < 4 else w1_t[i - 4]
                sp.dma_start(stage[:, i % 2], src).then_inc(stage_loaded[i % 2], 16)
            sp.wait_ge(pads_set, 1)
            sp.dma_start(keys_aug[BOT:BOT + 1, :], log_rel).then_inc(weights_loaded, 16)
            sp.dma_start(rk_aug[BOT:BOT + 1, :], log_rel).then_inc(weights_loaded, 16)
            sp.wait_ge(quad_used, 4 * FFN_TILES)
            sp.dma_start(wvu, wvu_t).then_inc(wvu_loaded, 16)
            with sp.Fori(0, BATCH) as b:
                sp.wait_ge(y_done, b * 2 + 2)
                sp.dma_start(out[bass.ds(b, 1)].rearrange("o p g h c -> (o p) (g h c)"),
                             x_sb[:, bass.ds(b * (2 * HID), 2 * HID)]).then_inc(s_out, 16)
            sp.wait_ge(s_out, 16 * BATCH)

        @block.gpsimd
        def _(pool):
            pool.memset(ident[:, :], 0.0).then_inc(s_const, 1)
            pool.wait_ge(s_const, 1)
            pool.affine_select(out=ident[:, :], in_=ident[:, :], compare_op=ALU.not_equal, fill=1.0,
                               base=0, pattern=[[-1, 128]], channel_multiplier=1).then_inc(s_ident, 1)
            pool.memset(minus_half[:, :], -0.5).then_inc(s_const, 1)
            pool.wait_ge(s_const, 2)
            pool.wait_ge(s_veps, 1)
            pool.tensor_tensor(rstd[:, :], veps[:, :], minus_half[:, :], ALU.pow).then_inc(s_rstd, 1)

            def step(pair, k, last):
                n = k + 2
                if n >= 0 and not (last and n >= PER_PAIR):
                    pool.wait_ge(exped, count(pair, 16, n + 1))
                    pool.tensor_tensor(p_lo[:, n % 4, :], p_sb[:, n % 4, :], high(p_sb[:, n % 4, :]),
                                       ALU.subtract).then_inc(p_split, 1)
                if k in (-7, 2, 10):
                    g = (k + 7) // 8 if k > 0 else 0
                    if not (last and g >= 2):
                        pool.wait_ge(v_hi_done, count(pair, 2, g + 1))
                        pool.tensor_tensor(v_lo[:, g % 2], v_raw[:, g % 2], v_hi[:, g % 2, :, 0:D],
                                           ALU.subtract).then_inc(v_split, 1)

            sweep(pool, step)

            pool.memset(half2[:, :], -0.5).then_inc(s_const, 1)
            pool.memset(ones[:, :], 1.0).then_inc(ones_set, 1)
            pool.wait_ge(s_const, 3)

            def norm(b, i):
                if in_range(b, i + 1):
                    pool.wait_ge(ve2_done, count(b, 2, i + 2))
                    if from_tile(b, i, 0):
                        pool.wait_ge(h_staged, count(b, 4, 2 * i + 2))
                    pool.tensor_tensor(rs2[:, :], ve2[:, :], half2[:, :], ALU.pow).then_inc(rs2_done, 1)

            sweep_tiles(pool, norm)

        @block.scalar
        def _(act):
            act.dma_start(tanh_gx[:, :], g_x).then_inc(s_gx, 16)
            act.dma_start(mask_sb[:, :, :], mask).then_inc(s_mask, 16)
            for b in range(1, BATCH):
                act.dma_start(x5[:, b], x[b]).then_inc(x_loaded[b], 16)
            act.wait_ge(s_gx, 16)
            act.activation(tanh_gx[:, :], tanh_gx[:, :], ACT.Tanh).then_inc(s_tanh, 1)

            def step(pair, k, last):
                h = {-7: 0, -3: 1}.get(k, (k - 2) // 4 + 2 if k >= 0 and k % 4 == 3 else None)
                if h is not None and not (last and h >= 4):
                    act.wait_ge(q_turned, count(pair, 4, h + 1))
                    act.activation(q_t[:, h % 2, :], mix_ps[:, (h + 1) % 2, 0:REP * HALF], ACT.Copy).then_inc(q_hi_done, 1)
                if k in (-8, 1, 9):
                    g = (k + 7) // 8 if k > 0 else 0
                    if not (last and g >= 2):
                        u = g % 2
                        act.wait_ge(k_loaded[u], count(pair, 32, 32 * (g // 2 + 1)))
                        if k > 0:
                            act.wait_ge(scored, count(pair, 16, 8 * g - 8 + (0 if k > 0 else 0)) if g else 0)
                        act.activation(k_hi[:, u, :], k_raw[:, u, :], ACT.Copy).then_inc(k_hi_done, 1)
                        act.wait_ge(v_loaded[u], count(pair, 16, 16 * (g // 2 + 1)))
                        if k > 0:
                            act.wait_ge(mixed, count(pair, 4, 2 * g - 2))
                        if k < 0:
                            act.wait_ge(s_init, 1)
                        act.activation(v_hi[:, u, :, 0:D], v_raw[:, u], ACT.Copy).then_inc(v_hi_done, 1)
                n = k + 3
                if shifts_on_act(n) and n >= 0 and not (last and n >= PER_PAIR):
                    act.wait_ge(maxed, count(pair, 16, n + 1))
                    act.activation(s_sb[:, n % 4, :], s_sb[:, n % 4, :], ACT.Identity, bias=row_max[:, n % 4, :],
                                   scale=-1.0).then_inc(shifted_a, 1)
                n = k + 2
                if n >= 0 and not (last and n >= PER_PAIR):
                    act.wait_ge(turned, count(pair, 16, n + 1))
                    act.activation(p_sb[:, n % 4, :].rearrange("p (a c) -> p a c", a=2),
                                   tr_ps[0:TC, :, 0:NCH // 2 * HALF], ACT.Exp,
                                   scale=-1.0 if shifts_on_act(n) else 1.0).then_inc(exped, 1)

            sweep(act, step)

            act.wait_ge(x_added, NHALF)
            act.wait_ge(weights_loaded, 48)
            act.activation(wq_cat[:, :, 0:BOT], wq_raw, ACT.Copy).then_inc(wq_hi_done, 1)
            act.wait_ge(rk_summed, 1)
            act.wait_ge(pads_set, 1)
            act.activation(keys_aug[0:BOT, :], keys_aug[0:BOT, :], ACT.Copy, scale=float(BOT) ** -0.5).then_inc(tables_ready, 1)
            act.activation(rk_aug[0:RDIM, :], psum[0:RDIM, 5, :], ACT.Copy, scale=float(RDIM) ** -0.5).then_inc(tables_ready, 1)
            for i in range(4):
                act.wait_ge(stage_loaded[i % 2], 16 * (3 + i // 2))
                act.activation(w1_hi[:, 4 * i:4 * i + 4, :], stage[:, i % 2], ACT.Copy).then_inc(w1_hi_done, 1)
            act.wait_ge(v2_piece, 4)
            act.activation(v2, psum[:, 4, :].rearrange("p (m n) -> p m n", m=4), ACT.Copy).then_inc(tables_ready, 1)
            act.wait_ge(w1_split, 4)

            def ffn(b, i):
                for j in range(4):
                    if in_range(b, i + 1):
                        act.wait_ge(h_turned, count(b, 8, 4 * (i + 1) + j + 1))
                        if from_tile(b, i, 0):
                            act.wait_ge(quad_used, count(b, 8, 4 * i + j + 1))
                        act.activation(h_hi[:, j], psum[:, j % 2, 0:4 * HALF].rearrange("p (k n) -> p k n", k=4),
                                       ACT.Copy).then_inc(h_hi_done, 1)
                    if in_range(b, i - 1) and j == 0:
                        act.wait_ge(rq_summed, count(b, 2, i))
                        act.activation(rq_aug[0:RDIM, :], psum[0:RDIM, 5, 0:HALF], ACT.Copy).then_inc(rq_ready, 1)
                    if in_range(b, i - 2) and j == 1:
                        act.wait_ge(z_summed, count(b, 2, i - 1))
                        act.activation(z_all[:, bass.ds(b * (2 * HALF) + (i - 2) * HALF, HALF)],
                                       psum[:, 7, 0:HALF], ACT.Copy).then_inc(z_ready, 1)
                    if in_range(b, i - 1) and j == 3:
                        act.wait_ge(selected, count(b, 2, i))
                        act.activation(w_rows, rest, ACT.Exp, bias=neg_top[:, :], accum_out=w_sum[:, :]).then_inc(weighed, 1)
                        act.wait_ge(w_turned, count(b, 2, i))
                        act.activation(w_t, psum[:, 6, 0:4 * HALF].rearrange("p (m n) -> p m n", m=4), ACT.Copy).then_inc(w_t_ready, 1)
                if in_range(b, i):
                    act.wait_ge(quad_used, count(b, 8, 4 * i + 4))
                    act.activation(q_tmp, psum[BOT:2 * BOT, 3, 0:HALF], ACT.Copy).then_inc(q_half, 1)
                    if from_tile(b, i, 1):
                        act.wait_ge(learned_summed, count(b, 2, i))
                    for f in range(4):
                        ins = act.activation(gelu_t[:, f, :], psum[:, 2, f * HALF:(f + 1) * HALF], ACT.Gelu_apprx_tanh,
                                             bias=bu1[:, f:f + 1])
                    ins.then_inc(gelu_done, 1)

            act.wait_ge(small_loaded, 64)
            sweep_tiles(act, ffn)

            act.activation(tanh_gf[:, :], scal[:, 0:1], ACT.Tanh).then_inc(gf_tanh, 1)
            act.wait_ge(gate_v, 1)
            act.activation(gate[:, 1, :], gate[:, 0, :], ACT.Ln, bias=1.0).then_inc(log_var_done, 1)
            act.wait_ge(gate_v, 3)
            act.activation(gate[:, 3, :], gate[:, 2, :], ACT.Exp, scale=-1.0).then_inc(gate_a, 1)
            act.wait_ge(gate_v, GATE_EXP)
            act.activation(gate[:, 3, :], gate[:, 2, :], ACT.Exp, scale=-1.0).then_inc(gate_a, 1)
            act.wait_ge(gate_v, GATE_BASE)

            def base(b, i):
                at = count(b, 2 * HALF, i * HALF)
                if not isinstance(b, int) or b > 0:
                    act.wait_ge(aux_summed, b * 2 + i - 1)
                act.activation(z_cur[:, i, :], z_all[:, bass.ds(at, HALF)], ACT.Copy).then_inc(z_copied, 1)
                act.activation(rows_of(b, i), rows_of(b, i), ACT.Identity, bias=gate[:, 9, bass.ds(b * 2 + i, 1)],
                               scale=gate[:, 8, bass.ds(b * 2 + i, 1)]).then_inc(base_done, 1)

            for i in range(2):
                base(0, i)
            with act.Fori(1, BATCH) as b:
                for i in range(2):
                    base(b, i)

        @block.tensor
        def _(pe):
            pe.wait_ge(s_ident, 1)

            def turn_q(pair, h):
                pe.wait_ge(q_staged, count(pair, 4, h + 1))
                if not isinstance(pair, int) or 4 * pair + h >= 3:
                    pe.wait_ge(x_added, count(pair, 4, h - 2))
                for r in range(REP):
                    mm = pe.transpose(mix_ps[:, (h + 1) % 2, r * HALF:(r + 1) * HALF],
                                      q_rows[:, h % 2, r].rearrange("p a d -> p (a d)"), ident[0:HALF, 0:HALF])
                mm.then_inc(q_turned, 1)

            def score(pair, n):
                h, u = n // 4, n // 8 % 2
                if n % 8 == 0:
                    pe.wait_ge(k_split, count(pair, 2, n // 8 + 1))
                if n % 4 == 0:
                    pe.wait_ge(q_split, count(pair, 4, h + 1))
                if not isinstance(pair, int) or n >= 2:
                    pe.wait_ge(maxed, count(pair, 16, n - 1))
                q = q_t[:, h % 2, (n % 4) * HALF:(n % 4 + 1) * HALF]
                for i, part in enumerate((k_hi, k_lo)):
                    for c in range(2):
                        mm = pe.matmul(score_ps[0:HALF, n % 2, c, 0:CTX // 2], q,
                                       part[:, u, c * (CTX // 2):(c + 1) * (CTX // 2)], start=(i == 0), stop=(i == 1))
                mm.then_inc(scored, 1)

            def turn(pair, n):
                if shifts_on_act(n):
                    pe.wait_ge(shifted_a, count(pair, 8, n // 2 + 1))
                else:
                    pe.wait_ge(shifted_v, count(pair, 8, n // 2 + 1))
                if not isinstance(pair, int) or n >= 1:
                    pe.wait_ge(exped, count(pair, 16, n))
                for c in range(NCH):
                    at = c % 3 * HALF
                    mm = pe.transpose(tr_ps[0:TC, c // 3, at:at + HALF], s_sb[:, n % 4, c * TC:(c + 1) * TC],
                                      ident[0:HALF, 0:HALF])
                mm.then_inc(turned, 1)

            def mix(pair, n, last):
                h, u = n // 4, n // 8 % 2
                if n % 8 == 0:
                    pe.wait_ge(v_split, count(pair, 2, n // 8 + 1))
                if n % 4 == 0 and not (last and h + 1 >= 4):
                    pe.wait_ge(q_split, count(pair, 4, h + 2))
                pe.wait_ge(p_split, count(pair, 16, n + 1))
                at = n % 4 * (D + 1)
                for c in range(NCH):
                    hi = high(p_sb[:, n % 4, c * HALF:(c + 1) * HALF])
                    lo = p_lo[:, n % 4, c * HALF:(c + 1) * HALF]
                    pe.matmul(mix_ps[0:HALF, h % 2, at:at + D + 1], hi, v_hi[:, u, c, :],
                              start=(c == 0), stop=False, skip_group_check=True)
                    pe.matmul(mix_ps[0:HALF, h % 2, at:at + D], hi, v_lo[:, u, c, :],
                              start=False, stop=False, skip_group_check=True)
                    mm = pe.matmul(mix_ps[0:HALF, h % 2, at:at + D + 1], lo, v_hi[:, u, c, :],
                                   start=False, stop=(c == NCH - 1), skip_group_check=True)
                if n % 4 == 3:
                    mm.then_inc(mixed, 1)

            def step(pair, k, last):
                n = k + 4
                if n >= 0 and not (last and n >= PER_PAIR):
                    score(pair, n)
                h = {-7: 0, -6: 1}.get(k, k // 4 + 2 if k >= 0 and k % 4 == 2 else None)
                if h is not None and not (last and h >= 4):
                    turn_q(pair, h)
                n = k + 2
                if n >= 0 and not (last and n >= PER_PAIR):
                    turn(pair, n)
                if k >= 0 and not (last and k >= PER_PAIR):
                    mix(pair, k, last)

            sweep(pe, step)

            pe.wait_ge(x_added, NHALF)
            pe.wait_ge(weights_loaded, 48)
            pe.wait_ge(small_loaded, 64)
            pe.matmul(psum[0:RDIM, 5, :], wr_t[0:BOT, :], keys_aug[0:BOT, :], start=True, stop=True).then_inc(rk_summed, 1)
            for i in range(4):
                pe.wait_ge(stage_loaded[i % 2], 16 * (1 + i // 2))
                for kk in range(4):
                    for m in range(4):
                        mm = pe.matmul(psum[:, 4, m * 128:(m + 1) * 128], stage[:, i % 2, kk, m * 128:(m + 1) * 128],
                                       wvd_sb[:, 4 * i + kk, :], start=(i == 0 and kk == 0 and m == 0),
                                       stop=(i == 3 and kk == 3), skip_group_check=True)
                mm.then_inc(v2_piece, 1)

            def turn_h(b, i, j):
                if j % 2 == 0:
                    pe.wait_ge(h_staged, count(b, 4, 2 * i + j // 2 + 1))
                if from_tile(b, i, 1) or j >= 2:
                    pe.wait_ge(h_split, count(b, 8, 4 * i + j - 1))
                for k in range(4):
                    mm = pe.transpose(psum[:, j % 2, k * HALF:(k + 1) * HALF],
                                      h_rows[:, j // 2, (j % 2 * 4 + k) * 128:(j % 2 * 4 + k + 1) * 128], ident[0:HALF, 0:HALF])
                mm.then_inc(h_turned, 1)

            def sum_quarter(b, i, j):
                pe.wait_ge(h_split, count(b, 8, 4 * i + j + 1))
                if j == 0 and from_tile(b, i, 1):
                    pe.wait_ge(gelu_done, count(b, 2, i))
                    pe.wait_ge(q_ready, count(b, 2, i))
                for kk in range(4):
                    k = 4 * j + kk
                    for f in range(4):
                        for n, (w, h) in enumerate(((w1_hi, h_hi), (w1_hi, h_lo), (w1_lo, h_hi))):
                            pe.matmul(psum[:, 2, f * HALF:(f + 1) * HALF], w[:, k, f * 128:(f + 1) * 128], h[:, j, kk, :],
                                      start=(k == 0 and f == 0 and n == 0), stop=(k == KC - 1), skip_group_check=True)
                    for n, h in enumerate((h_hi, h_lo)):
                        mm = pe.matmul(psum[:, 3, 0:HALF], wq_cat[:, k, :], h[:, j, kk, :], start=(k == 0 and n == 0),
                                       stop=(k == KC - 1 and n == 1))
                mm.then_inc(quad_used, 1)

            def ffn(b, i):
                for j in range(4):
                    if in_range(b, i):
                        sum_quarter(b, i, j)
                    if in_range(b, i + 1):
                        turn_h(b, i + 1, j)
                    if in_range(b, i - 1) and j == 0:
                        pe.wait_ge(q_ready, count(b, 2, i))
                        if from_tile(b, i, 2):
                            pe.wait_ge(selected, count(b, 2, i - 1))
                        pe.matmul(psum[0:RDIM, 5, 0:HALF], wr_t[:, :], q_aug, start=True, stop=True).then_inc(rq_summed, 1)
                    if in_range(b, i - 2) and j == 0:
                        pe.wait_ge(w_t_ready, count(b, 2, i - 1))
                        pe.wait_ge(learned_kept, count(b, 2, i - 1))
                        for m in range(4):
                            mm = pe.matmul(psum[:, 7, 0:HALF], v2[:, m, :], w_t[:, m, :], start=(m == 0), stop=(m == 3))
                        mm.then_inc(z_summed, 1)
                    if in_range(b, i - 1) and j == 1:
                        pe.wait_ge(rq_ready, count(b, 2, i))
                        pe.matmul(psum[0:HALF, 4, :], rq_aug, rk_aug, start=True, stop=True)
                        pe.matmul(psum[0:HALF, 5, :], q_aug, keys_aug, start=True, stop=True).then_inc(routed, 1)
                    if in_range(b, i - 1) and j == 2:
                        pe.wait_ge(gelu_done, count(b, 2, i))
                        if from_tile(b, i, 2):
                            pe.wait_ge(z_ready, count(b, 2, i - 1))
                        for f in range(4):
                            mm = pe.matmul(psum[0:HALF, 7, 511:512], gelu_t[:, f, :], wu2[:, f:f + 1], start=(f == 0), stop=(f == 3))
                        mm.then_inc(learned_summed, 1)
                    if in_range(b, i - 1) and j == 3:
                        pe.wait_ge(weighed, count(b, 2, i))
                        if from_tile(b, i, 2):
                            pe.wait_ge(w_t_ready, count(b, 2, i - 1))
                        for m in range(4):
                            mm = pe.transpose(psum[:, 6, m * HALF:(m + 1) * HALF], w_rows[:, m * 128:(m + 1) * 128],
                                              ident[0:HALF, 0:HALF])
                        mm.then_inc(w_turned, 1)

            pe.wait_ge(s_init, 2)
            pe.wait_ge(w1_split, 4)
            pe.wait_ge(wq_split, 1)
            pe.wait_ge(tables_ready, 3)
            pe.wait_ge(weights_loaded, 80)
            sweep_tiles(pe, ffn)

            pe.wait_ge(gate_v, 2)
            pe.wait_ge(ones_set, 1)
            pe.matmul(psum[0:HALF, 0, 0:1], ones[:, :], gate[:, 2, 0:1], start=True, stop=True).then_inc(mean_summed, 1)
            pe.wait_ge(gate_v, GATE_BASE)
            pe.wait_ge(wvu_loaded, 16)

            def aux(b, i):
                pe.wait_ge(z_copied, b * 2 + i + 1)
                if not isinstance(b, int) or b > 0:
                    pe.wait_ge(y_done, b * 2 + i - 1)
                for n in range(4):
                    mm = pe.matmul(psum[0:HALF, 4 * i + n, :], z_cur[:, i, :], wvu[:, n * 512:(n + 1) * 512], start=True, stop=True)
                mm.then_inc(aux_summed, 1)

            for i in range(2):
                aux(0, i)
            with pe.Fori(1, BATCH) as b:
                for i in range(2):
                    aux(b, i)

        @block.vector
        def _(dve):
            def wait_alone(s, value):
                dve.wait_ge(s, value)
                dve.sem_inc(passed, 1)

            dve.memset(v_hi[:, :, :, :], 1.0).then_inc(s_init, 1)
            dve.memset(wr_t[BOT:128, :], 0.0).then_inc(s_init, 1)
            for b in range(BATCH):
                dve.wait_ge(x_loaded[b], 16)
                if b:
                    dve.wait_ge(s_agg, 2 * b)
                for h in range(2):
                    for c in range(KV // 2):
                        bn = dve.bn_stats(stats[:, h, c, :], x5[:, b, 2 * c:2 * c + 2, h, :])
                bn.then_inc(s_bn, 1)
                dve.wait_ge(s_bn, b + 1)
                for h in range(2):
                    dve.bn_aggr(meanvar[:, 2 * b + h, :], stats[:, h, 0:4, :]).then_inc(s_agg, 1)
            dve.wait_ge(s_agg, 16)
            dve.tensor_scalar(veps[:, :], meanvar[:, :, 1], EPS, None, ALU.add).then_inc(s_veps, 1)
            dve.tensor_copy(ln_mean[:, :, :].rearrange("p (b g) h -> p b g h", b=BATCH),
                            meanvar[:, :, 0].rearrange("p (b h) -> p b h", b=BATCH).unsqueeze(2).broadcast_to([HALF, BATCH, 4, 2])
                            ).then_inc(s_ln, 1)
            dve.wait_ge(s_rstd, 1)
            dve.tensor_scalar(ln_scale[:, :, :].rearrange("p (b g) h -> p b g h", b=BATCH),
                              rstd[:, :].rearrange("p (b h) -> p b h", b=BATCH).unsqueeze(2).broadcast_to([HALF, BATCH, 4, 2]),
                              float(D) ** -0.5, None, ALU.mult).then_inc(s_ln, 1)
            dve.wait_ge(s_ln, 2)
            dve.wait_ge(s_mask, 16)
            dve.wait_ge(s_tanh, 1)

            def stage_q(pair, h):
                if not isinstance(pair, int) or h >= 2:
                    dve.wait_ge(q_turned, count(pair, 4, h - 1))
                src_pair = pair if h < 4 else pair + 1
                at = count(pair, 4 * GW, h * GW)
                mcol = ln_mean[:, :, :].rearrange("p a h -> p (a h)")[:, bass.ds(src_pair * 2 + h % 2, 1)]
                scol = ln_scale[:, :, :].rearrange("p a h -> p (a h)")[:, bass.ds(src_pair * 2 + h % 2, 1)]
                dve.tensor_scalar(q_rows[:, h % 2], x_sb[:, bass.ds(at, GW)].rearrange("p (r d) -> p r d", r=REP).unsqueeze(2).broadcast_to([HALF, REP, 2, D]),
                                  mcol, scol, ALU.subtract, ALU.mult).then_inc(q_staged, 1)

            def add_mix(pair, h):
                o = mix_ps[0:HALF, h % 2, 0:REP * (D + 1)].rearrange("p (r e) -> p r e", r=REP)
                dve.wait_ge(mixed, count(pair, 4, h + 1))
                dve.reciprocal(r_den[:, 0, :], o[:, :, D]).then_inc(den_done, 1)
                dve.wait_ge(den_done, count(pair, 8, 2 * h + 1))
                dve.tensor_scalar(r_den[:, 1, :], r_den[:, 0, :], tanh_gx[:, 0:1], None, ALU.mult).then_inc(den_done, 1)
                dve.wait_ge(den_done, count(pair, 8, 2 * h + 2))
                for r in range(REP):
                    xs = x_sb[:, bass.ds(count(pair, 4 * GW, h * GW + r * D), D)]
                    ins = dve.scalar_tensor_tensor(xs, o[:, r, 0:D], r_den[:, 1, r:r + 1], xs, ALU.mult, ALU.add)
                ins.then_inc(x_added, 1)

            def step(pair, k, last):
                h = {-8: 0, -7: 1}.get(k, k // 4 + 2 if k >= 0 and k % 4 == 1 else None)
                if h is not None and not (last and h >= 4):
                    stage_q(pair, h)
                h = {-6: 0, -3: 1}.get(k, (k - 2) // 4 + 2 if k >= 0 and k % 4 == 3 else None)
                if h is not None and not (last and h >= 4):
                    dve.wait_ge(q_hi_done, count(pair, 4, h + 1))
                    dve.tensor_tensor(q_t[D:2 * D, h % 2, :], mix_ps[D:2 * D, (h + 1) % 2, 0:REP * HALF],
                                      q_t[D:2 * D, h % 2, :], ALU.subtract).then_inc(q_split, 1)
                if k in (-8, 2, 10):
                    g = (k + 7) // 8 if k > 0 else 0
                    if not (last and g >= 2):
                        dve.wait_ge(k_hi_done, count(pair, 2, g + 1))
                        dve.tensor_tensor(k_lo[:, g % 2, :], k_raw[:, g % 2, :], k_hi[:, g % 2, :],
                                          ALU.subtract).then_inc(k_split, 1)
                n = k + 4
                if n >= 0 and not (last and n >= PER_PAIR):
                    wait_alone(scored, count(pair, 16, n + 1))
                    dve.tensor_tensor_reduce(
                        s_sb[:, n % 4, :].rearrange("p (a c) -> p a c", a=2), score_ps[0:HALF, n % 2, :, 0:CTX // 2],
                        mask_sb[:, n // 4 % 2, :].rearrange("p (a c) -> p a c", a=2), 1.0, -3.4e38,
                        ALU.add, ALU.max, row_max[:, n % 4, :]).then_inc(maxed, 1)
                n = k + 3
                if not shifts_on_act(n) and n >= 0 and not (last and n >= PER_PAIR):
                    dve.wait_ge(maxed, count(pair, 16, n + 1))
                    dve.tensor_scalar(s_sb[:, n % 4, :], s_sb[:, n % 4, :], row_max[:, n % 4, :], None,
                                      ALU.subtract).then_inc(shifted_v, 1)
                if k >= 0 and k % 4 == 3:
                    add_mix(pair, k // 4) if not (last and k >= PER_PAIR) else None

            sweep(dve, step)

            dve.wait_ge(x_added, NHALF)
            dve.memset(keys_aug[BOT:128, :], 0.0)
            dve.memset(rk_aug[:, :], 0.0).then_inc(pads_set, 1)
            dve.wait_ge(wq_hi_done, 1)
            dve.tensor_tensor(wq_cat[:, :, BOT:2 * BOT], wq_raw, wq_cat[:, :, 0:BOT], ALU.subtract).then_inc(wq_split, 1)
            for i in range(4):
                dve.wait_ge(w1_hi_done, i + 1)
                if i == 2:
                    dve.wait_ge(v2_piece, 4)
                dve.tensor_tensor(w1_lo[:, 4 * i:4 * i + 4, :], stage[:, i % 2], w1_hi[:, 4 * i:4 * i + 4, :],
                                  ALU.subtract).then_inc(w1_split, 1)
            dve.wait_ge(w1_split, 4)
            dve.memset(q_aug[BOT:128, :], 0.0).then_inc(pads_set, 1)
            dve.memset(rq_aug[:, :], 0.0).then_inc(pads_set, 1)
            dve.wait_ge(pads_set, 3)
            dve.memset(q_aug[BOT:BOT + 1, :], 1.0).then_inc(pads_set, 1)
            dve.memset(rq_aug[BOT:BOT + 1, :], 1.0).then_inc(pads_set, 1)
            dve.wait_ge(pads_set, 5)

            def stats_of(b, i):
                rows = rows_of(b, i)
                for c in range(4):
                    ins = dve.bn_stats(bn2[:, c, :], rows[:, 2 * c:2 * c + 2, :])
                ins.then_inc(bn2_done, 1)
                wait_alone(bn2_done, count(b, 2, i + 1))
                dve.bn_aggr(mv2[:, :], bn2[:, :, :]).then_inc(mv2_done, 1)
                dve.wait_ge(mv2_done, count(b, 2, i + 1))
                dve.tensor_scalar(ve2[:, :], mv2[:, 1:2], EPS, None, ALU.add).then_inc(ve2_done, 1)
                dve.tensor_copy(mean_all[:, bass.ds(b * 2 + i, 1)], mv2[:, 0:1])
                dve.tensor_copy(var_all[:, bass.ds(b * 2 + i, 1)], mv2[:, 1:2])
                dve.wait_ge(rs2_done, count(b, 2, i + 1))
                dve.tensor_copy(rstd_all[:, bass.ds(b * 2 + i, 1)], rs2[:, :])

            def stage_h(b, i, p):
                rows = rows_of(b, i)
                if from_tile(b, i, 1):
                    dve.wait_ge(h_turned, count(b, 8, 4 * (i - 1) + 2 * p + 2))
                dve.tensor_scalar(h_rows[:, p, :].rearrange("p (g c) -> p g c", g=4), rows[:, 4 * p:4 * p + 4, :],
                                  mv2[:, 0:1], rs2[:, :], ALU.subtract, ALU.mult).then_inc(h_staged, 1)

            def ffn(b, i):
                for j in range(4):
                    if in_range(b, i + 1) and i < 0 and j == 0:
                        stats_of(b, i + 1)
                        stage_h(b, i + 1, 0)
                        stage_h(b, i + 1, 1)
                    if in_range(b, i + 1):
                        dve.wait_ge(h_hi_done, count(b, 8, 4 * (i + 1) + j + 1))
                        dve.tensor_tensor(h_lo[:, j], psum[:, j % 2, 0:4 * HALF].rearrange("p (k n) -> p k n", k=4), h_hi[:, j],
                                          ALU.subtract).then_inc(h_split, 1)
                    if in_range(b, i + 2) and j == 1:
                        stats_of(b, i + 2)
                        stage_h(b, i + 2, 0)
                    if in_range(b, i + 2) and j == 3:
                        stage_h(b, i + 2, 1)
                    if in_range(b, i - 1) and j == 1:
                        pass
                    if in_range(b, i - 1) and j == 2:
                        router = psum[0:HALF, 4, :]
                        wait_alone(routed, count(b, 2, i))
                        dve.max(top8[:, :], router).then_inc(topped, 1)
                        wait_alone(topped, count(b, 6, 3 * i - 2))
                        dve.match_replace(unsel, top8[:, :], router, -3.0e38).then_inc(topped, 1)
                        dve.wait_ge(topped, count(b, 6, 3 * i - 1))
                        dve.tensor_tensor(unsel, router, unsel, ALU.is_equal).then_inc(topped, 1)
                        dve.wait_ge(topped, count(b, 6, 3 * i))
                        dve.scalar_tensor_tensor(rest, unsel, -1.0e30, psum[0:HALF, 5, :], ALU.mult, ALU.add).then_inc(logits_done, 1)
                        dve.wait_ge(logits_done, count(b, 2, i))
                        dve.tensor_reduce(neg_top[:, :], rest, AX.X, ALU.max, negate=True).then_inc(selected, 1)
                    if in_range(b, i - 1) and j == 3:
                        dve.wait_ge(learned_summed, count(b, 2, i))
                        dve.tensor_copy(learned[:, bass.ds(b * 2 + i - 1, 1)], psum[0:HALF, 7, 511:512]).then_inc(learned_kept, 1)
                        dve.wait_ge(weighed, count(b, 2, i))
                        dve.tensor_copy(wsum_all[:, bass.ds(b * 2 + i - 1, 1)], w_sum[:, :])
                if in_range(b, i):
                    dve.wait_ge(q_half, count(b, 2, i + 1))
                    dve.tensor_tensor(q_aug[0:BOT, :], psum[0:BOT, 3, 0:HALF], q_tmp, ALU.add).then_inc(q_ready, 1)

            sweep_tiles(dve, ffn)

            steps = [0]

            def gate_step(ins):
                steps[0] += 1
                ins.then_inc(gate_v, 1)
                dve.wait_ge(gate_v, steps[0])

            one = lambda n: gate[:, n, 0:1]
            dve.wait_ge(h_staged, 2 * FFN_TILES)
            dve.tensor_tensor(gate[:, 4, :], rstd_all[:, :], rstd_all[:, :], ALU.mult).then_inc(sq_done, 1)
            dve.wait_ge(sq_done, 1)
            gate_step(dve.tensor_tensor(gate[:, 0, :], var_all[:, :], gate[:, 4, :], ALU.mult))
            dve.wait_ge(log_var_done, 1)
            gate_step(dve.tensor_reduce(one(2), gate[:, 1, :], AX.X, ALU.add))
            dve.wait_ge(mean_summed, 1)
            dve.tensor_scalar(one(5), psum[0:HALF, 0, 0:1], 1.0 / ROWS, 1e-6, ALU.mult, ALU.add).then_inc(sq_done, 1)
            dve.wait_ge(sq_done, 2)
            dve.reciprocal(one(6), one(5)).then_inc(sq_done, 1)
            gate_step(dve.tensor_scalar(gate[:, 2, :], learned[:, :], scal[:, 3:4], None, ALU.add))
            dve.wait_ge(sq_done, 3)
            gate_step(dve.tensor_scalar(gate[:, 7, :], gate[:, 1, :], one(6), 0.5, ALU.mult, ALU.mult))
            dve.wait_ge(gate_a, 1)
            gate_step(dve.tensor_scalar(gate[:, 4, :], gate[:, 3, :], 1.0, None, ALU.add))
            gate_step(dve.reciprocal(gate[:, 5, :], gate[:, 4, :]))
            gate_step(dve.scalar_tensor_tensor(gate[:, 4, :], gate[:, 5, :], 2.5, gate[:, 7, :], ALU.mult, ALU.add))
            gate_step(dve.tensor_scalar(gate[:, 5, :], gate[:, 4, :], 0.0, 5.0, ALU.max, ALU.min))
            gate_step(dve.tensor_scalar(gate[:, 4, :], gate[:, 5, :], TAU_LOW, 1.0 / (TAU_HIGH - TAU_LOW), ALU.subtract, ALU.mult))
            gate_step(dve.tensor_scalar(gate[:, 5, :], gate[:, 4, :], 0.0, 1.0, ALU.max, ALU.min))
            gate_step(dve.tensor_scalar(gate[:, 2, :], gate[:, 5, :], scal[:, 1:2], scal[:, 2:3], ALU.mult, ALU.add))
            assert steps[0] == GATE_EXP
            dve.wait_ge(gate_a, 2)
            gate_step(dve.tensor_scalar(gate[:, 4, :], gate[:, 3, :], 1.0, None, ALU.add))
            gate_step(dve.reciprocal(gate[:, 5, :], gate[:, 4, :]))
            gate_step(dve.scalar_tensor_tensor(gate[:, 4, :], gate[:, 5, :], EARLY_EXIT, gate[:, 5, :], ALU.is_ge, ALU.mult))
            gate_step(dve.reciprocal(gate[:, 5, :], wsum_all[:, :]))
            dve.wait_ge(gf_tanh, 1)
            gate_step(dve.scalar_tensor_tensor(gate[:, 10, :], gate[:, 4, :], tanh_gf[:, :], gate[:, 5, :], ALU.mult, ALU.mult))
            gate_step(dve.tensor_scalar(gate[:, 7, :], rstd_all[:, :], tanh_gf[:, :], None, ALU.mult))
            gate_step(dve.tensor_scalar(gate[:, 8, :], gate[:, 7, :], 1.0, None, ALU.add))
            gate_step(dve.scalar_tensor_tensor(gate[:, 9, :], mean_all[:, :], -1.0, gate[:, 7, :], ALU.mult, ALU.mult))
            assert steps[0] == GATE_BASE

            def finish(b, i):
                rows = rows_of(b, i)
                dve.wait_ge(base_done, b * 2 + i + 1)
                dve.wait_ge(aux_summed, b * 2 + i + 1)
                for n in range(4):
                    part = rows[:, 2 * n:2 * n + 2, :]
                    ins = dve.scalar_tensor_tensor(part, psum[0:HALF, 4 * i + n, :].rearrange("p (g c) -> p g c", g=2),
                                                   gate[:, 10, bass.ds(b * 2 + i, 1)], part, ALU.mult, ALU.add)
                ins.then_inc(y_done, 1)

            with dve.Fori(0, BATCH) as b:
                for i in range(2):
                    finish(b, i)


_OUT = (BATCH, SEQ, HID)


def kernel(**inputs):
    import numpy as _np
    import concourse.bacc as _bacc
    from concourse import mybir as _mybir
    from concourse.bass_utils import run_bass_kernel_spmd as _run

    nc = _bacc.Bacc("TRN2", target_bir_lowering=False, num_devices=1)
    a = {k: _np.asarray(v) for k, v in inputs.items()}
    c = a["ctx_1024"]
    laid = {
        "x": a["x"].reshape(BATCH, 2, HALF, KV, GW).transpose(0, 2, 3, 1, 4),
        "k_t": c.transpose(0, 2, 1).reshape(GROUPS, D, CTX),
        "v_rows": c.reshape(BATCH, NCH, TC, KV, D).transpose(0, 3, 2, 1, 4).reshape(GROUPS, TC, NCH * D),
        "mask": a["mask_SxS2_ff0"].reshape(2, HALF, CTX).transpose(1, 0, 2),
        "g_x": _np.broadcast_to(a["g_xattn"].reshape(1, 1), (HALF, 1)),
        "av_t": a["L0_ffn_aux_values"].T.reshape(4, 4, 128, NSLOT).transpose(0, 2, 1, 3),
        "wvd_t": a["L0_ffn_Wvd"].T.reshape(KC, 128, VB).transpose(1, 0, 2),
        "w1_t": a["L0_ffn_Wu1"].T.reshape(4, 4, 128, F1).transpose(0, 2, 1, 3),
        "wq_t": a["L0_ffn_Wq"].T.reshape(KC, 128, BOT).transpose(1, 0, 2),
        "wr": a["L0_ffn_Wr"].T,
        "keys_t": a["L0_ffn_aux_keys"].T,
        "log_rel": a["L0_ffn_log_rel"].reshape(1, NSLOT),
        "b1": a["L0_ffn_bu1"].reshape(4, 128).T,
        "w2": a["L0_ffn_Wu2"].reshape(4, 128).T,
        "wvu_t": a["L0_ffn_Wvu"].T,
        "scalars": _np.broadcast_to(_np.concatenate([a[n].reshape(1) for n in (
            "g_ffn", "L0_ffn_gate_w1", "L0_ffn_gate_bias", "L0_ffn_bu2")]).reshape(1, 4), (HALF, 4)),
    }
    arrays, args = {}, []
    for name, v in laid.items():
        v = _np.ascontiguousarray(v)
        arrays[f"in_{name}"] = v
        args.append(nc.dram_tensor(f"in_{name}", v.shape, _mybir.dt.from_np(v.dtype), kind="ExternalInput").ap())
    o = nc.dram_tensor("out_0", (BATCH, HALF, KV, 2, GW), F32, kind="ExternalOutput").ap()
    flamingo_block(nc, *args, o)
    r = _run(nc, [arrays], core_ids=[0])
    got = r.results[0]["out_0"].reshape(BATCH, HALF, KV, 2, GW).transpose(0, 3, 1, 2, 4).reshape(_OUT)
    return _np.ascontiguousarray(got)
```

```python
from contextlib import ExitStack

import concourse.bass as bass
from concourse import mybir

ALU = mybir.AluOpType
ACT = mybir.ActivationFunctionType
AX = mybir.AxisListType
F32 = mybir.dt.float32
BF16 = mybir.dt.bfloat16

BATCH, SEQ, HID = 8, 224, 2048
CTX, CDIM = 750, 512
HEADS, KV = 32, 8
REP = HEADS // KV
D = HID // HEADS
HALF = SEQ // 2
NCH = 6
TC = CTX // NCH
GROUPS = BATCH * KV
NHALF = 2 * GROUPS
TILES = NHALF * REP
PAIRS = GROUPS // 2
PER_PAIR = 2 * 2 * REP
GW = REP * D
EPS = 1e-5
BOT, RDIM, NSLOT, TOPK, VB, F1 = 64, 48, 512, 8, 128, HID // 4
KC = HID // 128
FFN_TILES = 2 * BATCH
ROWS = BATCH * SEQ
TAU_LOW, TAU_HIGH, EARLY_EXIT = 0.5, 2.0, 0.05
ARENA = 19280
STAGE_SLOTS = 3
V2_TURNS = {(0, 3): range(0, 2), (1, 0): range(2, 5), (1, 1): range(5, 8)}
GATE_EXP = 11
GATE_BASE = 19


def high(ap):
    return ap.bitcast(BF16)[..., 1::2]


def flamingo_block(nc, x, k_t, v_rows, mask, g_x, av_t, wvd_t, w1_t, wq_t, wr, keys_t, log_rel, b1, w2, wvu_t, scalars, out):
    with ExitStack() as ctx:
        def sb(name, shape, dt=F32):
            return ctx.enter_context(nc.sbuf_tensor(name, shape, dt))

        def pb(name, shape):
            return ctx.enter_context(nc.psum_tensor(name, shape, F32))

        def sem(name):
            return ctx.enter_context(nc.semaphore(name))

        x_sb = sb("x_sb", [HALF, GROUPS * 2 * GW])
        x5 = x_sb[:, :].rearrange("p (b g h c) -> p b g h c", b=BATCH, g=KV, h=2)
        ident = sb("ident", [128, 128])
        tanh_gx = sb("tanh_gx", [HALF, 1])
        stats = sb("stats", [HALF, 2, KV, 6])
        meanvar = sb("meanvar", [HALF, 16, 2])
        veps = sb("veps", [HALF, 16])
        minus_half = sb("minus_half", [HALF, 16])
        rstd = sb("rstd", [HALF, 16])
        ln_mean = sb("ln_mean", [HALF, PAIRS, 2])
        ln_scale = sb("ln_scale", [HALF, PAIRS, 2])

        arena = sb("arena", [128, ARENA])
        used = {"attention": 0, "ffn": 0}

        def carve(phase, shape, dt=F32):
            words = 1
            for n in shape[1:]:
                words *= n
            words = words * (2 if dt == BF16 else 4) // 4
            at = used[phase]
            used[phase] = at + words
            assert used[phase] <= ARENA, (phase, used[phase])
            ap = arena[0:shape[0], at:at + words]
            ap = ap.bitcast(BF16) if dt == BF16 else ap
            if len(shape) == 3:
                ap = ap.rearrange("p (a b) -> p a b", a=shape[1])
            elif len(shape) == 4:
                ap = ap.rearrange("p (a b c) -> p a b c", a=shape[1], b=shape[2])
            elif len(shape) == 5:
                ap = ap.rearrange("p (a b c d) -> p a b c d", a=shape[1], b=shape[2], c=shape[3])
            return ap

        mask_sb = carve("attention", [HALF, 2, CTX])
        k_raw = carve("attention", [128, 2, CTX])
        k_hi = carve("attention", [128, 2, CTX], BF16)
        k_lo = carve("attention", [128, 2, CTX], BF16)
        v_raw = carve("attention", [TC, 2, NCH, D])
        v_hi = carve("attention", [TC, 2, NCH, D + 1], BF16)
        v_lo = carve("attention", [TC, 2, NCH, D], BF16)
        q_rows = carve("attention", [HALF, 2, REP, 2, D])
        q_t = carve("attention", [128, 2, REP * HALF], BF16)
        s_sb = carve("attention", [HALF, 4, CTX])
        row_max = carve("attention", [HALF, 4, 1])
        p_sb = carve("attention", [TC, 4, NCH * HALF])
        p_lo = carve("attention", [TC, 4, NCH * HALF], BF16)
        r_den = carve("attention", [HALF, 2, REP])

        w1_hi = carve("ffn", [128, KC, F1], BF16)
        w1_lo = carve("ffn", [128, KC, F1], BF16)
        wq_cat = carve("ffn", [128, KC, 2 * BOT], BF16)
        h_rows = carve("ffn", [HALF, 2, 2 * GW])
        h_hi = carve("ffn", [128, 4, 4, HALF], BF16)
        h_lo = carve("ffn", [128, 4, 4, HALF], BF16)
        keys_aug = carve("ffn", [128, NSLOT])
        rk_aug = carve("ffn", [128, NSLOT])
        v2 = carve("ffn", [128, 4, VB])
        b1_rows = carve("ffn", [HALF, F1])
        w2_rows = carve("ffn", [HALF, F1])
        stage_at = used["ffn"]
        z_all = carve("ffn", [128, 2 * BATCH * HALF])
        w_rows = carve("ffn", [HALF, NSLOT])
        w_t = carve("ffn", [128, 4, HALF])
        logits = carve("ffn", [HALF, NSLOT])
        unsel = carve("ffn", [HALF, NSLOT])
        used["ffn"] = stage_at + STAGE_SLOTS * (2 * NSLOT + 2 * VB)
        q_aug = carve("ffn", [128, HALF])
        rq_aug = carve("ffn", [128, HALF])
        q_tmp = carve("ffn", [64, HALF])
        g_rows = carve("ffn", [HALF, F1])
        wvu = arena[:, 0:HID]
        z_cur = arena[:, HID:HID + 2 * HALF].rearrange("p (h c) -> p h c", h=2)

        assert used["attention"] <= stage_at
        stage = arena[:, stage_at:stage_at + 2 * 4 * F1].rearrange("p (s k n) -> p s k n", s=2, k=4)
        slots = arena[:, stage_at:stage_at + STAGE_SLOTS * (2 * NSLOT + 2 * VB)].rearrange("p (s n) -> p s n", s=STAGE_SLOTS)
        av_stage = slots[:, :, 0:2 * NSLOT].rearrange("p s (k n) -> p s k n", k=2)
        wvd_stage = slots[:, :, 2 * NSLOT:2 * NSLOT + 2 * VB].rearrange("p s (k n) -> p s k n", k=2)
        wq_raw = arena[:, 9216:9216 + KC * BOT].rearrange("p (k n) -> p k n", k=KC)
        wr_t = sb("wr_t", [128, RDIM])
        scal = sb("scal", [HALF, 4])
        tanh_gf = sb("tanh_gf", [HALF, 1])
        ones = sb("ones", [HALF, HALF])
        bn2 = sb("bn2", [HALF, 4, 6])
        mv2 = sb("mv2", [HALF, 2])
        ve2 = sb("ve2", [HALF, 1])
        half2 = sb("half2", [HALF, 1])
        rs2 = sb("rs2", [HALF, 1])
        top8 = sb("top8", [HALF, 8])
        neg_top = sb("neg_top", [HALF, 1])
        w_sum = sb("w_sum", [HALF, 1])
        dot = sb("dot", [HALF, 1])
        mean_all = sb("mean_all", [HALF, FFN_TILES])
        var_all = sb("var_all", [HALF, FFN_TILES])
        rstd_all = sb("rstd_all", [HALF, FFN_TILES])
        wsum_all = sb("wsum_all", [HALF, FFN_TILES])
        learned = sb("learned", [HALF, FFN_TILES])
        gate = sb("gate", [HALF, 12, FFN_TILES])

        psum = pb("psum", [128, 8, 512])
        score_ps = psum[:, 0:4, :].rearrange("p (s c) n -> p s c n", s=2)
        tr_ps = psum[:, 4:6, :]
        mix_ps = psum[:, 6:8, :]

        s_const = sem("s_const")
        s_ident = sem("s_ident")
        s_init = sem("s_init")
        s_gx = sem("s_gx")
        s_tanh = sem("s_tanh")
        x_loaded = [sem(f"x_loaded{b}") for b in range(BATCH)]
        s_mask = sem("s_mask")
        s_bn = sem("s_bn")
        s_agg = sem("s_agg")
        s_rstd = sem("s_rstd")
        s_veps = sem("s_veps")
        s_ln = sem("s_ln")
        k_loaded = [sem("k_loaded0"), sem("k_loaded1")]
        v_loaded = [sem("v_loaded0"), sem("v_loaded1")]
        k_hi_done = sem("k_hi_done")
        k_split = sem("k_split")
        v_hi_done = sem("v_hi_done")
        v_split = sem("v_split")
        q_staged = sem("q_staged")
        q_turned = sem("q_turned")
        q_hi_done = sem("q_hi_done")
        q_split = sem("q_split")
        scored = sem("scored")
        passed = sem("passed")
        maxed = sem("maxed")
        shifted_v = sem("shifted_v")
        shifted_a = sem("shifted_a")
        turned = sem("turned")
        exped = sem("exped")
        p_split = sem("p_split")
        mixed = sem("mixed")
        den_done = sem("den_done")
        x_added = sem("x_added")
        s_out = sem("s_out")

        stage_loaded = [sem("stage_loaded0"), sem("stage_loaded1")]
        weights_loaded = sem("weights_loaded")
        rows_loaded = sem("rows_loaded")
        rel_loaded = sem("rel_loaded")
        v2_loaded = [sem(f"v2_loaded{i}") for i in range(STAGE_SLOTS)]
        v2_ready = sem("v2_ready")
        preact_done = sem("preact_done")
        dotted = sem("dotted")
        small_loaded = sem("small_loaded")
        pads_set = sem("pads_set")
        v2_piece = sem("v2_piece")
        w1_hi_done = sem("w1_hi_done")
        w1_split = sem("w1_split")
        wq_hi_done = sem("wq_hi_done")
        wq_split = sem("wq_split")
        rk_summed = sem("rk_summed")
        tables_ready = sem("tables_ready")
        bn2_done = sem("bn2_done")
        mv2_done = sem("mv2_done")
        ve2_done = sem("ve2_done")
        rs2_done = sem("rs2_done")
        logits_done = sem("logits_done")
        sq_done = sem("sq_done")
        h_staged = sem("h_staged")
        h_turned = sem("h_turned")
        h_hi_done = sem("h_hi_done")
        h_split = sem("h_split")
        quad_used = sem("quad_used")
        q_half = sem("q_half")
        q_ready = sem("q_ready")
        rq_summed = sem("rq_summed")
        rq_ready = sem("rq_ready")
        routed = sem("routed")
        topped = sem("topped")
        selected = sem("selected")
        weighed = sem("weighed")
        w_turned = sem("w_turned")
        w_t_ready = sem("w_t_ready")
        z_summed = sem("z_summed")
        z_ready = sem("z_ready")
        gelu_done = sem("gelu_done")
        ones_set = sem("ones_set")
        wvu_loaded = sem("wvu_loaded")
        gf_tanh = sem("gf_tanh")
        log_var_done = sem("log_var_done")
        mean_summed = sem("mean_summed")
        gate_v = sem("gate_v")
        gate_a = sem("gate_a")
        z_copied = sem("z_copied")
        aux_summed = sem("aux_summed")
        base_done = sem("base_done")
        y_done = sem("y_done")

        block = ctx.enter_context(nc.Block())

        def shifts_on_act(k):
            return k % 2 == 1

        def sweep(eng, step):
            for k in range(-8, 0):
                step(0, k, False)
            with eng.Fori(0, PAIRS - 1) as pair:
                for k in range(PER_PAIR):
                    step(pair, k, False)
            for k in range(PER_PAIR + 2):
                step(PAIRS - 1, k, True)

        def sweep_tiles(eng, step):
            for i in (-1, 0, 1):
                step(0, i)
            with eng.Fori(1, BATCH - 1) as b:
                for i in range(2):
                    step(b, i)
            for i in range(4):
                step(BATCH - 1, i)

        def in_range(b, i):
            return not isinstance(b, int) or 0 <= 2 * b + i < FFN_TILES

        def from_tile(b, i, first):
            return not isinstance(b, int) or 2 * b + i >= first

        def rows_of(b, i):
            flat = x_sb[:, bass.ds(b * (2 * HID) + i // 2 * (2 * HID), 2 * HID)]
            return flat.rearrange("p (g h c) -> p g h c", g=KV, h=2)[:, :, i % 2, :]

        def count(pair, per_pair, local):
            return pair * per_pair + local

        @block.sync
        def _(sp):
            sp.dma_start(x5[:, 0], x[0]).then_inc(x_loaded[0], 16)

            def load(pair, u):
                g = count(pair, 2, u)
                for part in range(2):
                    sp.dma_start(k_raw[D * part:D * part + D, u, :], k_t[bass.ds(g, 1)].rearrange("o d t -> (o d) t")).then_inc(k_loaded[u], 16)
                sp.dma_start(v_raw[:, u], v_rows[bass.ds(g, 1)].rearrange("o p (c d) -> (o p) c d", c=NCH)).then_inc(v_loaded[u], 16)

            load(0, 0)
            load(0, 1)
            for i in range(2):
                sp.dma_start(stage[:, i], w1_t[i]).then_inc(stage_loaded[i], 16)
            for dst, src in ((wr_t[0:BOT], wr), (scal, scalars)):
                sp.dma_start(dst[:], src).then_inc(small_loaded, 16)
            with sp.Fori(1, PAIRS) as pair:
                for u in range(2):
                    sp.wait_ge(k_split, count(pair, 2, u - 1))
                    sp.wait_ge(v_split, count(pair, 2, u - 1))
                    load(pair, u)
            sp.wait_ge(x_added, NHALF)
            sp.dma_start(keys_aug[0:BOT, :], keys_t).then_inc(weights_loaded, 16)
            sp.dma_start(wq_raw, wq_t).then_inc(weights_loaded, 16)
            sp.dma_start(b1_rows, b1).then_inc(rows_loaded, 16)
            sp.dma_start(w2_rows, w2).then_inc(rows_loaded, 16)
            for i in range(2, 4):
                sp.wait_ge(w1_split, i - 1)
                sp.dma_start(stage[:, i % 2], w1_t[i]).then_inc(stage_loaded[i % 2], 16)
            sp.wait_ge(pads_set, 1)
            sp.dma_start(keys_aug[BOT:BOT + 1, :], log_rel).then_inc(rel_loaded, 16)
            sp.dma_start(rk_aug[BOT:BOT + 1, :], log_rel).then_inc(rel_loaded, 16)
            sp.wait_ge(w1_split, 4)
            for i in range(KC // 2):
                if i >= STAGE_SLOTS:
                    sp.wait_ge(v2_piece, i - STAGE_SLOTS + 1)
                slot = i % STAGE_SLOTS
                sp.dma_start(av_stage[:, slot], av_t[i]).then_inc(v2_loaded[slot], 16)
                sp.dma_start(wvd_stage[:, slot], wvd_t[i]).then_inc(v2_loaded[slot], 16)
            sp.wait_ge(quad_used, 4 * FFN_TILES)
            sp.dma_start(wvu, wvu_t).then_inc(wvu_loaded, 16)
            with sp.Fori(0, BATCH) as b:
                sp.wait_ge(y_done, b * 2 + 2)
                sp.dma_start(out[bass.ds(b, 1)].rearrange("o p g h c -> (o p) (g h c)"),
                             x_sb[:, bass.ds(b * (2 * HID), 2 * HID)]).then_inc(s_out, 16)
            sp.wait_ge(s_out, 16 * BATCH)

        @block.gpsimd
        def _(pool):
            pool.memset(ident[:, :], 0.0).then_inc(s_const, 1)
            pool.wait_ge(s_const, 1)
            pool.affine_select(out=ident[:, :], in_=ident[:, :], compare_op=ALU.not_equal, fill=1.0,
                               base=0, pattern=[[-1, 128]], channel_multiplier=1).then_inc(s_ident, 1)
            pool.memset(minus_half[:, :], -0.5).then_inc(s_const, 1)
            pool.wait_ge(s_const, 2)
            pool.wait_ge(s_veps, 1)
            pool.tensor_tensor(rstd[:, :], veps[:, :], minus_half[:, :], ALU.pow).then_inc(s_rstd, 1)

            def step(pair, k, last):
                n = k + 2
                if n >= 0 and not (last and n >= PER_PAIR):
                    pool.wait_ge(exped, count(pair, 16, n + 1))
                    pool.tensor_tensor(p_lo[:, n % 4, :], p_sb[:, n % 4, :], high(p_sb[:, n % 4, :]),
                                       ALU.subtract).then_inc(p_split, 1)
                if k in (-7, 2, 10):
                    g = (k + 7) // 8 if k > 0 else 0
                    if not (last and g >= 2):
                        pool.wait_ge(v_hi_done, count(pair, 2, g + 1))
                        pool.tensor_tensor(v_lo[:, g % 2], v_raw[:, g % 2], v_hi[:, g % 2, :, 0:D],
                                           ALU.subtract).then_inc(v_split, 1)

            sweep(pool, step)

            pool.memset(half2[:, :], -0.5).then_inc(s_const, 1)
            pool.memset(ones[:, :], 1.0).then_inc(ones_set, 1)
            pool.wait_ge(s_const, 3)

            def norm(b, i):
                if in_range(b, i + 1):
                    pool.wait_ge(ve2_done, count(b, 2, i + 2))
                    if from_tile(b, i, 0):
                        pool.wait_ge(h_staged, count(b, 8, 4 * i + 4))
                    pool.tensor_tensor(rs2[:, :], ve2[:, :], half2[:, :], ALU.pow).then_inc(rs2_done, 1)

            sweep_tiles(pool, norm)

        @block.scalar
        def _(act):
            act.dma_start(tanh_gx[:, :], g_x).then_inc(s_gx, 16)
            act.dma_start(mask_sb[:, :, :], mask).then_inc(s_mask, 16)
            for b in range(1, BATCH):
                act.dma_start(x5[:, b], x[b]).then_inc(x_loaded[b], 16)
            act.wait_ge(s_gx, 16)
            act.activation(tanh_gx[:, :], tanh_gx[:, :], ACT.Tanh).then_inc(s_tanh, 1)

            def step(pair, k, last):
                h = {-7: 0, -3: 1}.get(k, (k - 2) // 4 + 2 if k >= 0 and k % 4 == 3 else None)
                if h is not None and not (last and h >= 4):
                    act.wait_ge(q_turned, count(pair, 4, h + 1))
                    act.activation(q_t[:, h % 2, :], mix_ps[:, (h + 1) % 2, 0:REP * HALF], ACT.Copy).then_inc(q_hi_done, 1)
                if k in (-8, 1, 9):
                    g = (k + 7) // 8 if k > 0 else 0
                    if not (last and g >= 2):
                        u = g % 2
                        act.wait_ge(k_loaded[u], count(pair, 32, 32 * (g // 2 + 1)))
                        if k > 0:
                            act.wait_ge(scored, count(pair, 16, 8 * g - 8 + (0 if k > 0 else 0)) if g else 0)
                        act.activation(k_hi[:, u, :], k_raw[:, u, :], ACT.Copy).then_inc(k_hi_done, 1)
                        act.wait_ge(v_loaded[u], count(pair, 16, 16 * (g // 2 + 1)))
                        if k > 0:
                            act.wait_ge(mixed, count(pair, 4, 2 * g - 2))
                        if k < 0:
                            act.wait_ge(s_init, 1)
                        act.activation(v_hi[:, u, :, 0:D], v_raw[:, u], ACT.Copy).then_inc(v_hi_done, 1)
                n = k + 3
                if shifts_on_act(n) and n >= 0 and not (last and n >= PER_PAIR):
                    act.wait_ge(maxed, count(pair, 16, n + 1))
                    act.activation(s_sb[:, n % 4, :], s_sb[:, n % 4, :], ACT.Identity, bias=row_max[:, n % 4, :],
                                   scale=-1.0).then_inc(shifted_a, 1)
                n = k + 2
                if n >= 0 and not (last and n >= PER_PAIR):
                    act.wait_ge(turned, count(pair, 16, n + 1))
                    act.activation(p_sb[:, n % 4, :].rearrange("p (a c) -> p a c", a=2),
                                   tr_ps[0:TC, :, 0:NCH // 2 * HALF], ACT.Exp,
                                   scale=-1.0 if shifts_on_act(n) else 1.0).then_inc(exped, 1)

            sweep(act, step)

            act.wait_ge(x_added, NHALF)
            for i in range(4):
                act.wait_ge(stage_loaded[i % 2], 16 * (1 + i // 2))
                act.activation(w1_hi[:, 4 * i:4 * i + 4, :], stage[:, i % 2], ACT.Copy).then_inc(w1_hi_done, 1)
                if i == 1:
                    act.wait_ge(weights_loaded, 32)
                    act.activation(wq_cat[:, :, 0:BOT], wq_raw, ACT.Copy).then_inc(wq_hi_done, 1)
                    act.wait_ge(rk_summed, 1)
                    act.wait_ge(pads_set, 1)
                    act.activation(keys_aug[0:BOT, :], keys_aug[0:BOT, :], ACT.Copy, scale=float(BOT) ** -0.5).then_inc(tables_ready, 1)
                    act.activation(rk_aug[0:RDIM, :], psum[0:RDIM, 5, :], ACT.Copy, scale=float(RDIM) ** -0.5).then_inc(tables_ready, 1)

            def ffn(b, i):
                for j in range(4):
                    if in_range(b, i + 1):
                        act.wait_ge(h_turned, count(b, 8, 4 * (i + 1) + j + 1))
                        if from_tile(b, i, 0):
                            act.wait_ge(quad_used, count(b, 8, 4 * i + j + 1))
                        act.activation(h_hi[:, j], psum[:, j % 2, 0:4 * HALF].rearrange("p (k n) -> p k n", k=4),
                                       ACT.Copy).then_inc(h_hi_done, 1)
                    if in_range(b, i - 1) and j == 0:
                        act.wait_ge(rq_summed, count(b, 2, i))
                        act.activation(rq_aug[0:RDIM, :], psum[0:RDIM, 5, 0:HALF], ACT.Copy).then_inc(rq_ready, 1)
                    if in_range(b, i - 2) and j == 1:
                        act.wait_ge(z_summed, count(b, 2, i - 1))
                        act.activation(z_all[:, bass.ds(b * (2 * HALF) + (i - 2) * HALF, HALF)],
                                       psum[:, 6, 0:HALF], ACT.Copy).then_inc(z_ready, 1)
                    if isinstance(b, int) and 2 * b + i == 1 and j == 1:
                        act.wait_ge(v2_piece, KC // 2)
                        act.activation(v2, psum[:, 6, :].rearrange("p (m n) -> p m n", m=4), ACT.Copy).then_inc(v2_ready, 1)
                    if in_range(b, i - 1) and j == 3:
                        act.wait_ge(selected, count(b, 2, i))
                        act.activation(w_rows, logits, ACT.Exp, bias=neg_top[:, :], accum_out=w_sum[:, :]).then_inc(weighed, 1)
                        act.wait_ge(w_turned, count(b, 2, i))
                        act.activation(w_t, psum[:, 6, 0:4 * HALF].rearrange("p (m n) -> p m n", m=4), ACT.Copy).then_inc(w_t_ready, 1)
                if in_range(b, i):
                    act.wait_ge(quad_used, count(b, 8, 4 * i + 4))
                    act.activation(q_tmp, psum[BOT:2 * BOT, 3, 0:HALF], ACT.Copy).then_inc(q_half, 1)
                    act.wait_ge(preact_done, count(b, 2, i + 1))
                    act.activation(g_rows, g_rows, ACT.Gelu_apprx_tanh).then_inc(gelu_done, 1)

            act.wait_ge(small_loaded, 32)
            sweep_tiles(act, ffn)

            act.activation(tanh_gf[:, :], scal[:, 0:1], ACT.Tanh).then_inc(gf_tanh, 1)
            act.wait_ge(gate_v, 1)
            act.activation(gate[:, 1, :], gate[:, 0, :], ACT.Ln, bias=1.0).then_inc(log_var_done, 1)
            act.wait_ge(gate_v, 3)
            act.activation(gate[:, 3, :], gate[:, 2, :], ACT.Exp, scale=-1.0).then_inc(gate_a, 1)
            act.wait_ge(gate_v, GATE_EXP)
            act.activation(gate[:, 3, :], gate[:, 2, :], ACT.Exp, scale=-1.0).then_inc(gate_a, 1)
            act.wait_ge(gate_v, GATE_BASE)

            def base(b, i):
                at = count(b, 2 * HALF, i * HALF)
                if not isinstance(b, int) or b > 0:
                    act.wait_ge(aux_summed, b * 2 + i - 1)
                act.activation(z_cur[:, i, :], z_all[:, bass.ds(at, HALF)], ACT.Copy).then_inc(z_copied, 1)
                act.activation(rows_of(b, i), rows_of(b, i), ACT.Identity, bias=gate[:, 9, bass.ds(b * 2 + i, 1)],
                               scale=gate[:, 8, bass.ds(b * 2 + i, 1)]).then_inc(base_done, 1)

            for i in range(2):
                base(0, i)
            with act.Fori(1, BATCH) as b:
                for i in range(2):
                    base(b, i)

        @block.tensor
        def _(pe):
            pe.wait_ge(s_ident, 1)

            def turn_q(pair, h):
                pe.wait_ge(q_staged, count(pair, 4, h + 1))
                if not isinstance(pair, int) or 4 * pair + h >= 3:
                    pe.wait_ge(x_added, count(pair, 4, h - 2))
                for r in range(REP):
                    mm = pe.transpose(mix_ps[:, (h + 1) % 2, r * HALF:(r + 1) * HALF],
                                      q_rows[:, h % 2, r].rearrange("p a d -> p (a d)"), ident[0:HALF, 0:HALF])
                mm.then_inc(q_turned, 1)

            def score(pair, n):
                h, u = n // 4, n // 8 % 2
                if n % 8 == 0:
                    pe.wait_ge(k_split, count(pair, 2, n // 8 + 1))
                if n % 4 == 0:
                    pe.wait_ge(q_split, count(pair, 4, h + 1))
                if not isinstance(pair, int) or n >= 2:
                    pe.wait_ge(maxed, count(pair, 16, n - 1))
                q = q_t[:, h % 2, (n % 4) * HALF:(n % 4 + 1) * HALF]
                for i, part in enumerate((k_hi, k_lo)):
                    for c in range(2):
                        mm = pe.matmul(score_ps[0:HALF, n % 2, c, 0:CTX // 2], q,
                                       part[:, u, c * (CTX // 2):(c + 1) * (CTX // 2)], start=(i == 0), stop=(i == 1))
                mm.then_inc(scored, 1)

            def turn(pair, n):
                if shifts_on_act(n):
                    pe.wait_ge(shifted_a, count(pair, 8, n // 2 + 1))
                else:
                    pe.wait_ge(shifted_v, count(pair, 8, n // 2 + 1))
                if not isinstance(pair, int) or n >= 1:
                    pe.wait_ge(exped, count(pair, 16, n))
                for c in range(NCH):
                    at = c % 3 * HALF
                    mm = pe.transpose(tr_ps[0:TC, c // 3, at:at + HALF], s_sb[:, n % 4, c * TC:(c + 1) * TC],
                                      ident[0:HALF, 0:HALF])
                mm.then_inc(turned, 1)

            def mix(pair, n, last):
                h, u = n // 4, n // 8 % 2
                if n % 8 == 0:
                    pe.wait_ge(v_split, count(pair, 2, n // 8 + 1))
                if n % 4 == 0 and not (last and h + 1 >= 4):
                    pe.wait_ge(q_split, count(pair, 4, h + 2))
                pe.wait_ge(p_split, count(pair, 16, n + 1))
                at = n % 4 * (D + 1)
                for c in range(NCH):
                    hi = high(p_sb[:, n % 4, c * HALF:(c + 1) * HALF])
                    lo = p_lo[:, n % 4, c * HALF:(c + 1) * HALF]
                    pe.matmul(mix_ps[0:HALF, h % 2, at:at + D + 1], hi, v_hi[:, u, c, :],
                              start=(c == 0), stop=False, skip_group_check=True)
                    pe.matmul(mix_ps[0:HALF, h % 2, at:at + D], hi, v_lo[:, u, c, :],
                              start=False, stop=False, skip_group_check=True)
                    mm = pe.matmul(mix_ps[0:HALF, h % 2, at:at + D + 1], lo, v_hi[:, u, c, :],
                                   start=False, stop=(c == NCH - 1), skip_group_check=True)
                if n % 4 == 3:
                    mm.then_inc(mixed, 1)

            def step(pair, k, last):
                n = k + 4
                if n >= 0 and not (last and n >= PER_PAIR):
                    score(pair, n)
                h = {-7: 0, -6: 1}.get(k, k // 4 + 2 if k >= 0 and k % 4 == 2 else None)
                if h is not None and not (last and h >= 4):
                    turn_q(pair, h)
                n = k + 2
                if n >= 0 and not (last and n >= PER_PAIR):
                    turn(pair, n)
                if k >= 0 and not (last and k >= PER_PAIR):
                    mix(pair, k, last)

            sweep(pe, step)

            pe.wait_ge(x_added, NHALF)
            pe.wait_ge(weights_loaded, 32)
            pe.wait_ge(small_loaded, 32)
            pe.matmul(psum[0:RDIM, 5, :], wr_t[0:BOT, :], keys_aug[0:BOT, :], start=True, stop=True).then_inc(rk_summed, 1)
            def sum_v2(pieces):
                for i in pieces:
                    pe.wait_ge(v2_loaded[i % STAGE_SLOTS], 32 * (1 + i // STAGE_SLOTS))
                    for kk in range(2):
                        for m in range(4):
                            mm = pe.matmul(psum[:, 6, m * 128:(m + 1) * 128], av_stage[:, i % STAGE_SLOTS, kk, m * 128:(m + 1) * 128],
                                           wvd_stage[:, i % STAGE_SLOTS, kk, :], start=(i == 0 and kk == 0 and m == 0),
                                           stop=(i == KC // 2 - 1 and kk == 1), skip_group_check=True)
                    mm.then_inc(v2_piece, 1)

            def turn_h(b, i, j):
                pe.wait_ge(h_staged, count(b, 8, 4 * i + j + 1))
                if from_tile(b, i, 1) or j >= 2:
                    pe.wait_ge(h_split, count(b, 8, 4 * i + j - 1))
                for k in range(4):
                    mm = pe.transpose(psum[:, j % 2, k * HALF:(k + 1) * HALF],
                                      h_rows[:, j % 2, k * 128:(k + 1) * 128], ident[0:HALF, 0:HALF])
                mm.then_inc(h_turned, 1)

            def sum_quarter(b, i, j):
                pe.wait_ge(h_split, count(b, 8, 4 * i + j + 1))
                if isinstance(b, int) and 2 * b + i == 0:
                    pe.wait_ge(w1_split, j + 1)
                if j == 0 and from_tile(b, i, 2):
                    pe.wait_ge(preact_done, count(b, 2, i - 1))
                for kk in range(4):
                    k = 4 * j + kk
                    for n, (h, w) in enumerate(((h_hi, w1_hi), (h_hi, w1_lo), (h_lo, w1_hi))):
                        pe.matmul(psum[0:HALF, 2 if i % 2 == 0 else 7, :], h[:, j, kk, :], w[:, k, :],
                                  start=(k == 0 and n == 0), stop=(k == KC - 1 and n == 2))
                if isinstance(b, int) and 2 * b + i == 0 and j == 0:
                    pe.wait_ge(wq_split, 1)
                if j == 0 and from_tile(b, i, 1):
                    pe.wait_ge(q_ready, count(b, 2, i))
                for kk in range(4):
                    k = 4 * j + kk
                    for n, h in enumerate((h_hi, h_lo)):
                        mm = pe.matmul(psum[:, 3, 0:HALF], wq_cat[:, k, :], h[:, j, kk, :], start=(k == 0 and n == 0),
                                       stop=(k == KC - 1 and n == 1))
                mm.then_inc(quad_used, 1)

            def ffn(b, i):
                for j in range(4):
                    if in_range(b, i):
                        sum_quarter(b, i, j)
                    if in_range(b, i + 1):
                        turn_h(b, i + 1, j)
                    if isinstance(b, int) and (2 * b + i, j) in V2_TURNS:
                        sum_v2(V2_TURNS[2 * b + i, j])
                    if in_range(b, i - 1) and j == 0:
                        pe.wait_ge(q_ready, count(b, 2, i))
                        if from_tile(b, i, 2):
                            pe.wait_ge(selected, count(b, 2, i - 1))
                        pe.matmul(psum[0:RDIM, 5, 0:HALF], wr_t[:, :], q_aug, start=True, stop=True).then_inc(rq_summed, 1)
                    if in_range(b, i - 2) and j == 0:
                        pe.wait_ge(w_t_ready, count(b, 2, i - 1))
                        if isinstance(b, int):
                            pe.wait_ge(v2_ready, 1)
                        for m in range(4):
                            mm = pe.matmul(psum[:, 6, 0:HALF], v2[:, m, :], w_t[:, m, :], start=(m == 0), stop=(m == 3))
                        mm.then_inc(z_summed, 1)
                    if in_range(b, i - 1) and j == 1:
                        pe.wait_ge(rq_ready, count(b, 2, i))
                        if isinstance(b, int) and 2 * b + i == 1:
                            pe.wait_ge(tables_ready, 2)
                            pe.wait_ge(rel_loaded, 32)
                        pe.matmul(psum[0:HALF, 4, :], rq_aug, rk_aug, start=True, stop=True)
                        pe.matmul(psum[0:HALF, 5, :], q_aug, keys_aug, start=True, stop=True).then_inc(routed, 1)
                    if in_range(b, i - 1) and j == 3:
                        pe.wait_ge(weighed, count(b, 2, i))
                        if isinstance(b, int) and 2 * b + i == 1:
                            pe.wait_ge(v2_ready, 1)
                        if from_tile(b, i, 2):
                            pe.wait_ge(z_ready, count(b, 2, i - 1))
                        for m in range(4):
                            mm = pe.transpose(psum[:, 6, m * HALF:(m + 1) * HALF], w_rows[:, m * 128:(m + 1) * 128],
                                              ident[0:HALF, 0:HALF])
                        mm.then_inc(w_turned, 1)

            pe.wait_ge(s_init, 2)
            sweep_tiles(pe, ffn)

            pe.wait_ge(gate_v, 2)
            pe.wait_ge(ones_set, 1)
            pe.matmul(psum[0:HALF, 0, 0:1], ones[:, :], gate[:, 2, 0:1], start=True, stop=True).then_inc(mean_summed, 1)
            pe.wait_ge(gate_v, GATE_BASE)
            pe.wait_ge(wvu_loaded, 16)

            def aux(b, i):
                pe.wait_ge(z_copied, b * 2 + i + 1)
                if not isinstance(b, int) or b > 0:
                    pe.wait_ge(y_done, b * 2 + i - 1)
                for n in range(4):
                    mm = pe.matmul(psum[0:HALF, 4 * i + n, :], z_cur[:, i, :], wvu[:, n * 512:(n + 1) * 512], start=True, stop=True)
                mm.then_inc(aux_summed, 1)

            for i in range(2):
                aux(0, i)
            with pe.Fori(1, BATCH) as b:
                for i in range(2):
                    aux(b, i)

        @block.vector
        def _(dve):
            def wait_alone(s, value):
                dve.wait_ge(s, value)
                dve.sem_inc(passed, 1)

            dve.memset(v_hi[:, :, :, :], 1.0).then_inc(s_init, 1)
            dve.memset(wr_t[BOT:128, :], 0.0).then_inc(s_init, 1)
            for b in range(BATCH):
                dve.wait_ge(x_loaded[b], 16)
                if b:
                    dve.wait_ge(s_agg, 2 * b)
                for h in range(2):
                    for c in range(KV // 2):
                        bn = dve.bn_stats(stats[:, h, c, :], x5[:, b, 2 * c:2 * c + 2, h, :])
                bn.then_inc(s_bn, 1)
                dve.wait_ge(s_bn, b + 1)
                for h in range(2):
                    dve.bn_aggr(meanvar[:, 2 * b + h, :], stats[:, h, 0:4, :]).then_inc(s_agg, 1)
            dve.wait_ge(s_agg, 16)
            dve.tensor_scalar(veps[:, :], meanvar[:, :, 1], EPS, None, ALU.add).then_inc(s_veps, 1)
            dve.tensor_copy(ln_mean[:, :, :].rearrange("p (b g) h -> p b g h", b=BATCH),
                            meanvar[:, :, 0].rearrange("p (b h) -> p b h", b=BATCH).unsqueeze(2).broadcast_to([HALF, BATCH, 4, 2])
                            ).then_inc(s_ln, 1)
            dve.wait_ge(s_rstd, 1)
            dve.tensor_scalar(ln_scale[:, :, :].rearrange("p (b g) h -> p b g h", b=BATCH),
                              rstd[:, :].rearrange("p (b h) -> p b h", b=BATCH).unsqueeze(2).broadcast_to([HALF, BATCH, 4, 2]),
                              float(D) ** -0.5, None, ALU.mult).then_inc(s_ln, 1)
            dve.wait_ge(s_ln, 2)
            dve.wait_ge(s_mask, 16)
            dve.wait_ge(s_tanh, 1)

            def stage_q(pair, h):
                if not isinstance(pair, int) or h >= 2:
                    dve.wait_ge(q_turned, count(pair, 4, h - 1))
                src_pair = pair if h < 4 else pair + 1
                at = count(pair, 4 * GW, h * GW)
                mcol = ln_mean[:, :, :].rearrange("p a h -> p (a h)")[:, bass.ds(src_pair * 2 + h % 2, 1)]
                scol = ln_scale[:, :, :].rearrange("p a h -> p (a h)")[:, bass.ds(src_pair * 2 + h % 2, 1)]
                dve.tensor_scalar(q_rows[:, h % 2], x_sb[:, bass.ds(at, GW)].rearrange("p (r d) -> p r d", r=REP).unsqueeze(2).broadcast_to([HALF, REP, 2, D]),
                                  mcol, scol, ALU.subtract, ALU.mult).then_inc(q_staged, 1)

            def add_mix(pair, h):
                o = mix_ps[0:HALF, h % 2, 0:REP * (D + 1)].rearrange("p (r e) -> p r e", r=REP)
                dve.wait_ge(mixed, count(pair, 4, h + 1))
                dve.reciprocal(r_den[:, 0, :], o[:, :, D]).then_inc(den_done, 1)
                dve.wait_ge(den_done, count(pair, 8, 2 * h + 1))
                dve.tensor_scalar(r_den[:, 1, :], r_den[:, 0, :], tanh_gx[:, 0:1], None, ALU.mult).then_inc(den_done, 1)
                dve.wait_ge(den_done, count(pair, 8, 2 * h + 2))
                for r in range(REP):
                    xs = x_sb[:, bass.ds(count(pair, 4 * GW, h * GW + r * D), D)]
                    ins = dve.scalar_tensor_tensor(xs, o[:, r, 0:D], r_den[:, 1, r:r + 1], xs, ALU.mult, ALU.add)
                ins.then_inc(x_added, 1)

            def step(pair, k, last):
                h = {-8: 0, -7: 1}.get(k, k // 4 + 2 if k >= 0 and k % 4 == 1 else None)
                if h is not None and not (last and h >= 4):
                    stage_q(pair, h)
                h = {-6: 0, -3: 1}.get(k, (k - 2) // 4 + 2 if k >= 0 and k % 4 == 3 else None)
                if h is not None and not (last and h >= 4):
                    dve.wait_ge(q_hi_done, count(pair, 4, h + 1))
                    dve.tensor_tensor(q_t[D:2 * D, h % 2, :], mix_ps[D:2 * D, (h + 1) % 2, 0:REP * HALF],
                                      q_t[D:2 * D, h % 2, :], ALU.subtract).then_inc(q_split, 1)
                if k in (-8, 2, 10):
                    g = (k + 7) // 8 if k > 0 else 0
                    if not (last and g >= 2):
                        dve.wait_ge(k_hi_done, count(pair, 2, g + 1))
                        dve.tensor_tensor(k_lo[:, g % 2, :], k_raw[:, g % 2, :], k_hi[:, g % 2, :],
                                          ALU.subtract).then_inc(k_split, 1)
                n = k + 4
                if n >= 0 and not (last and n >= PER_PAIR):
                    wait_alone(scored, count(pair, 16, n + 1))
                    dve.tensor_tensor_reduce(
                        s_sb[:, n % 4, :].rearrange("p (a c) -> p a c", a=2), score_ps[0:HALF, n % 2, :, 0:CTX // 2],
                        mask_sb[:, n // 4 % 2, :].rearrange("p (a c) -> p a c", a=2), 1.0, -3.4e38,
                        ALU.add, ALU.max, row_max[:, n % 4, :]).then_inc(maxed, 1)
                n = k + 3
                if not shifts_on_act(n) and n >= 0 and not (last and n >= PER_PAIR):
                    dve.wait_ge(maxed, count(pair, 16, n + 1))
                    dve.tensor_scalar(s_sb[:, n % 4, :], s_sb[:, n % 4, :], row_max[:, n % 4, :], None,
                                      ALU.subtract).then_inc(shifted_v, 1)
                if k >= 0 and k % 4 == 3:
                    add_mix(pair, k // 4) if not (last and k >= PER_PAIR) else None

            sweep(dve, step)

            dve.wait_ge(x_added, NHALF)
            dve.memset(keys_aug[BOT:128, :], 0.0)
            dve.memset(rk_aug[:, :], 0.0).then_inc(pads_set, 1)

            def split_w1(i):
                dve.wait_ge(w1_hi_done, i + 1)
                dve.tensor_tensor(w1_lo[:, 4 * i:4 * i + 4, :], stage[:, i % 2], w1_hi[:, 4 * i:4 * i + 4, :],
                                  ALU.subtract).then_inc(w1_split, 1)

            def stats_of(b, i):
                rows = rows_of(b, i)
                for c in range(4):
                    ins = dve.bn_stats(bn2[:, c, :], rows[:, 2 * c:2 * c + 2, :])
                ins.then_inc(bn2_done, 1)
                wait_alone(bn2_done, count(b, 2, i + 1))
                dve.bn_aggr(mv2[:, :], bn2[:, :, :]).then_inc(mv2_done, 1)
                dve.wait_ge(mv2_done, count(b, 2, i + 1))
                dve.tensor_scalar(ve2[:, :], mv2[:, 1:2], EPS, None, ALU.add).then_inc(ve2_done, 1)
                dve.tensor_copy(mean_all[:, bass.ds(b * 2 + i, 1)], mv2[:, 0:1])
                dve.tensor_copy(var_all[:, bass.ds(b * 2 + i, 1)], mv2[:, 1:2])
                dve.wait_ge(rs2_done, count(b, 2, i + 1))
                dve.tensor_copy(rstd_all[:, bass.ds(b * 2 + i, 1)], rs2[:, :])

            def stage_h(b, i, j):
                rows = rows_of(b, i)
                if from_tile(b, i, 1) or j >= 2:
                    dve.wait_ge(h_turned, count(b, 8, 4 * i + j - 1))
                dve.tensor_scalar(h_rows[:, j % 2, :].rearrange("p (g c) -> p g c", g=2), rows[:, 2 * j:2 * j + 2, :],
                                  mv2[:, 0:1], rs2[:, :], ALU.subtract, ALU.mult).then_inc(h_staged, 1)

            def ffn(b, i):
                first = isinstance(b, int) and i < 0
                if first:
                    stats_of(b, 0)
                    split_w1(0)
                    split_w1(1)
                    dve.wait_ge(wq_hi_done, 1)
                    dve.tensor_tensor(wq_cat[:, :, BOT:2 * BOT], wq_raw, wq_cat[:, :, 0:BOT], ALU.subtract).then_inc(wq_split, 1)
                    dve.wait_ge(wq_split, 1)
                    stage_h(b, 0, 0)
                    stage_h(b, 0, 1)
                for j in range(4):
                    if in_range(b, i + 1):
                        dve.wait_ge(h_hi_done, count(b, 8, 4 * (i + 1) + j + 1))
                        dve.tensor_tensor(h_lo[:, j], psum[:, j % 2, 0:4 * HALF].rearrange("p (k n) -> p k n", k=4), h_hi[:, j],
                                          ALU.subtract).then_inc(h_split, 1)
                        if j < 2:
                            stage_h(b, i + 1, j + 2)
                    if first and j < 2:
                        split_w1(2 + j)
                    if first and j == 1:
                        dve.wait_ge(w1_split, 4)
                        dve.memset(q_aug[BOT:128, :], 0.0).then_inc(pads_set, 1)
                        dve.memset(rq_aug[:, :], 0.0).then_inc(pads_set, 1)
                        dve.wait_ge(pads_set, 3)
                        dve.memset(q_aug[BOT:BOT + 1, :], 1.0).then_inc(pads_set, 1)
                        dve.memset(rq_aug[BOT:BOT + 1, :], 1.0).then_inc(pads_set, 1)
                        dve.wait_ge(pads_set, 5)
                    if in_range(b, i + 2) and j == 1:
                        stats_of(b, i + 2)
                    if in_range(b, i + 2) and j >= 2:
                        stage_h(b, i + 2, j - 2)
                    if in_range(b, i - 1) and j == 0:
                        dve.wait_ge(gelu_done, count(b, 2, i))
                        dve.sem_inc(passed, 1)
                        dve.tensor_tensor_reduce(g_rows, g_rows, w2_rows, 1.0, 0.0, ALU.mult, ALU.add, dot[:, :]).then_inc(dotted, 1)
                        dve.wait_ge(dotted, count(b, 2, i))
                        dve.tensor_copy(learned[:, bass.ds(b * 2 + i - 1, 1)], dot[:, :])
                    if in_range(b, i - 1) and j == 2:
                        router = psum[0:HALF, 4, :]
                        if isinstance(b, int) and 2 * b + i == 1:
                            dve.wait_ge(v2_piece, KC // 2)
                        wait_alone(routed, count(b, 2, i))
                        dve.max(top8[:, :], router).then_inc(topped, 1)
                        wait_alone(topped, count(b, 6, 3 * i - 2))
                        dve.match_replace(unsel, top8[:, :], router, -3.0e38).then_inc(topped, 1)
                        dve.wait_ge(topped, count(b, 6, 3 * i - 1))
                        dve.tensor_tensor(unsel, router, unsel, ALU.is_equal).then_inc(topped, 1)
                        dve.wait_ge(topped, count(b, 6, 3 * i))
                        dve.scalar_tensor_tensor(logits, unsel, -1.0e30, psum[0:HALF, 5, :], ALU.mult, ALU.add).then_inc(logits_done, 1)
                        dve.wait_ge(logits_done, count(b, 2, i))
                        dve.tensor_reduce(neg_top[:, :], logits, AX.X, ALU.max, negate=True).then_inc(selected, 1)
                    if in_range(b, i - 1) and j == 3:
                        dve.wait_ge(weighed, count(b, 2, i))
                        dve.tensor_copy(wsum_all[:, bass.ds(b * 2 + i - 1, 1)], w_sum[:, :])
                if in_range(b, i):
                    dve.wait_ge(q_half, count(b, 2, i + 1))
                    dve.tensor_tensor(q_aug[0:BOT, :], psum[0:BOT, 3, 0:HALF], q_tmp, ALU.add).then_inc(q_ready, 1)
                    if isinstance(b, int) and 2 * b + i == 0:
                        dve.wait_ge(rows_loaded, 32)
                    dve.tensor_tensor(g_rows, psum[0:HALF, 2 if i % 2 == 0 else 7, :], b1_rows, ALU.add).then_inc(preact_done, 1)

            sweep_tiles(dve, ffn)

            steps = [0]

            def gate_step(ins):
                steps[0] += 1
                ins.then_inc(gate_v, 1)
                dve.wait_ge(gate_v, steps[0])

            one = lambda n: gate[:, n, 0:1]
            dve.wait_ge(h_staged, 2 * FFN_TILES)
            dve.tensor_tensor(gate[:, 4, :], rstd_all[:, :], rstd_all[:, :], ALU.mult).then_inc(sq_done, 1)
            dve.wait_ge(sq_done, 1)
            gate_step(dve.tensor_tensor(gate[:, 0, :], var_all[:, :], gate[:, 4, :], ALU.mult))
            dve.wait_ge(log_var_done, 1)
            gate_step(dve.tensor_reduce(one(2), gate[:, 1, :], AX.X, ALU.add))
            dve.wait_ge(mean_summed, 1)
            dve.tensor_scalar(one(5), psum[0:HALF, 0, 0:1], 1.0 / ROWS, 1e-6, ALU.mult, ALU.add).then_inc(sq_done, 1)
            dve.wait_ge(sq_done, 2)
            dve.reciprocal(one(6), one(5)).then_inc(sq_done, 1)
            gate_step(dve.tensor_scalar(gate[:, 2, :], learned[:, :], scal[:, 3:4], None, ALU.add))
            dve.wait_ge(sq_done, 3)
            gate_step(dve.tensor_scalar(gate[:, 7, :], gate[:, 1, :], one(6), 0.5, ALU.mult, ALU.mult))
            dve.wait_ge(gate_a, 1)
            gate_step(dve.tensor_scalar(gate[:, 4, :], gate[:, 3, :], 1.0, None, ALU.add))
            gate_step(dve.reciprocal(gate[:, 5, :], gate[:, 4, :]))
            gate_step(dve.scalar_tensor_tensor(gate[:, 4, :], gate[:, 5, :], 2.5, gate[:, 7, :], ALU.mult, ALU.add))
            gate_step(dve.tensor_scalar(gate[:, 5, :], gate[:, 4, :], 0.0, 5.0, ALU.max, ALU.min))
            gate_step(dve.tensor_scalar(gate[:, 4, :], gate[:, 5, :], TAU_LOW, 1.0 / (TAU_HIGH - TAU_LOW), ALU.subtract, ALU.mult))
            gate_step(dve.tensor_scalar(gate[:, 5, :], gate[:, 4, :], 0.0, 1.0, ALU.max, ALU.min))
            gate_step(dve.tensor_scalar(gate[:, 2, :], gate[:, 5, :], scal[:, 1:2], scal[:, 2:3], ALU.mult, ALU.add))
            assert steps[0] == GATE_EXP
            dve.wait_ge(gate_a, 2)
            gate_step(dve.tensor_scalar(gate[:, 4, :], gate[:, 3, :], 1.0, None, ALU.add))
            gate_step(dve.reciprocal(gate[:, 5, :], gate[:, 4, :]))
            gate_step(dve.scalar_tensor_tensor(gate[:, 4, :], gate[:, 5, :], EARLY_EXIT, gate[:, 5, :], ALU.is_ge, ALU.mult))
            gate_step(dve.reciprocal(gate[:, 5, :], wsum_all[:, :]))
            dve.wait_ge(gf_tanh, 1)
            gate_step(dve.scalar_tensor_tensor(gate[:, 10, :], gate[:, 4, :], tanh_gf[:, :], gate[:, 5, :], ALU.mult, ALU.mult))
            gate_step(dve.tensor_scalar(gate[:, 7, :], rstd_all[:, :], tanh_gf[:, :], None, ALU.mult))
            gate_step(dve.tensor_scalar(gate[:, 8, :], gate[:, 7, :], 1.0, None, ALU.add))
            gate_step(dve.scalar_tensor_tensor(gate[:, 9, :], mean_all[:, :], -1.0, gate[:, 7, :], ALU.mult, ALU.mult))
            assert steps[0] == GATE_BASE

            def finish(b, i):
                rows = rows_of(b, i)
                dve.wait_ge(base_done, b * 2 + i + 1)
                dve.wait_ge(aux_summed, b * 2 + i + 1)
                for n in range(4):
                    part = rows[:, 2 * n:2 * n + 2, :]
                    ins = dve.scalar_tensor_tensor(part, psum[0:HALF, 4 * i + n, :].rearrange("p (g c) -> p g c", g=2),
                                                   gate[:, 10, bass.ds(b * 2 + i, 1)], part, ALU.mult, ALU.add)
                ins.then_inc(y_done, 1)

            with dve.Fori(0, BATCH) as b:
                for i in range(2):
                    finish(b, i)


_OUT = (BATCH, SEQ, HID)


def kernel(**inputs):
    import numpy as _np
    import concourse.bacc as _bacc
    from concourse import mybir as _mybir
    from concourse.bass_utils import run_bass_kernel_spmd as _run

    nc = _bacc.Bacc("TRN2", target_bir_lowering=False, num_devices=1)
    a = {k: _np.asarray(v) for k, v in inputs.items()}
    c = a["ctx_1024"]
    laid = {
        "x": a["x"].reshape(BATCH, 2, HALF, KV, GW).transpose(0, 2, 3, 1, 4),
        "k_t": c.transpose(0, 2, 1).reshape(GROUPS, D, CTX),
        "v_rows": c.reshape(BATCH, NCH, TC, KV, D).transpose(0, 3, 2, 1, 4).reshape(GROUPS, TC, NCH * D),
        "mask": a["mask_SxS2_ff0"].reshape(2, HALF, CTX).transpose(1, 0, 2),
        "g_x": _np.broadcast_to(a["g_xattn"].reshape(1, 1), (HALF, 1)),
        "av_t": a["L0_ffn_aux_values"].T.reshape(KC // 2, 2, 128, NSLOT).transpose(0, 2, 1, 3),
        "wvd_t": a["L0_ffn_Wvd"].T.reshape(KC // 2, 2, 128, VB).transpose(0, 2, 1, 3),
        "w1_t": a["L0_ffn_Wu1"].T.reshape(4, 4, 128, F1).transpose(0, 2, 1, 3),
        "wq_t": a["L0_ffn_Wq"].T.reshape(KC, 128, BOT).transpose(1, 0, 2),
        "wr": a["L0_ffn_Wr"].T,
        "keys_t": a["L0_ffn_aux_keys"].T,
        "log_rel": a["L0_ffn_log_rel"].reshape(1, NSLOT),
        "b1": _np.broadcast_to(a["L0_ffn_bu1"].reshape(1, F1), (HALF, F1)),
        "w2": _np.broadcast_to(a["L0_ffn_Wu2"].reshape(1, F1), (HALF, F1)),
        "wvu_t": a["L0_ffn_Wvu"].T,
        "scalars": _np.broadcast_to(_np.concatenate([a[n].reshape(1) for n in (
            "g_ffn", "L0_ffn_gate_w1", "L0_ffn_gate_bias", "L0_ffn_bu2")]).reshape(1, 4), (HALF, 4)),
    }
    arrays, args = {}, []
    for name, v in laid.items():
        v = _np.ascontiguousarray(v)
        arrays[f"in_{name}"] = v
        args.append(nc.dram_tensor(f"in_{name}", v.shape, _mybir.dt.from_np(v.dtype), kind="ExternalInput").ap())
    o = nc.dram_tensor("out_0", (BATCH, HALF, KV, 2, GW), F32, kind="ExternalOutput").ap()
    flamingo_block(nc, *args, o)
    r = _run(nc, [arrays], core_ids=[0])
    got = r.results[0]["out_0"].reshape(BATCH, HALF, KV, 2, GW).transpose(0, 3, 1, 2, 4).reshape(_OUT)
    return _np.ascontiguousarray(got)
```

```python
from contextlib import ExitStack

import concourse.bass as bass
from concourse import mybir

ALU = mybir.AluOpType
ACT = mybir.ActivationFunctionType
AX = mybir.AxisListType
F32 = mybir.dt.float32
BF16 = mybir.dt.bfloat16

BATCH, SEQ, HID = 8, 224, 2048
CTX, CDIM = 750, 512
HEADS, KV = 32, 8
REP = HEADS // KV
D = HID // HEADS
HALF = SEQ // 2
NCH = 6
TC = CTX // NCH
GROUPS = BATCH * KV
NHALF = 2 * GROUPS
PAIRS = GROUPS // 2
PER_PAIR = 2 * 2 * REP
PAIRS_A_BATCH = PAIRS // BATCH
GW = REP * D
EPS = 1e-5
BOT, RDIM, NSLOT, TOPK, VB, F1 = 64, 48, 512, 8, 128, HID // 4
KC = HID // 128
FFN_TILES = 2 * BATCH
ROWS = BATCH * SEQ
TAU_LOW, TAU_HIGH, EARLY_EXIT = 0.5, 2.0, 0.05
ARENA = 19280
STAGE_SLOTS = 3
V2_TURNS = {(0, 3): range(0, 2), (1, 0): range(2, 5), (1, 1): range(5, 8)}
GATE_EXP = 11
GATE_BASE = 19


def high(ap):
    return ap.bitcast(BF16)[..., 1::2]


def flamingo_block(nc, x, k_t, v_rows, mask, g_x, av_t, wvd_t, w1_t, wq_t, wr, keys_t, log_rel, b1, w2, wvu_t, scalars, out):
    with ExitStack() as ctx:
        def sb(name, shape, dt=F32):
            return ctx.enter_context(nc.sbuf_tensor(name, shape, dt))

        def pb(name, shape):
            return ctx.enter_context(nc.psum_tensor(name, shape, F32))

        def sem(name):
            return ctx.enter_context(nc.semaphore(name))

        x_sb = sb("x_sb", [HALF, GROUPS * 2 * GW])
        ident = sb("ident", [128, 128])
        tanh_gx = sb("tanh_gx", [HALF, 1])
        stats = sb("stats", [HALF, 2, PAIRS, 6])
        window = sb("window", [HALF, 2, PAIRS_A_BATCH, 6])
        meanvar = sb("meanvar", [HALF, 2, 2])
        veps = sb("veps", [HALF, 2])
        minus_half = sb("minus_half", [HALF, 2])
        rstd = sb("rstd", [HALF, 2])
        ln_mean = sb("ln_mean", [HALF, PAIRS, 2])
        ln_scale = sb("ln_scale", [HALF, PAIRS, 2])

        arena = sb("arena", [128, ARENA])
        used = {"attention": 0, "ffn": 0}

        def carve(phase, shape, dt=F32):
            words = 1
            for n in shape[1:]:
                words *= n
            words = words * (2 if dt == BF16 else 4) // 4
            at = used[phase]
            used[phase] = at + words
            assert used[phase] <= ARENA, (phase, used[phase])
            ap = arena[0:shape[0], at:at + words]
            ap = ap.bitcast(BF16) if dt == BF16 else ap
            if len(shape) == 3:
                ap = ap.rearrange("p (a b) -> p a b", a=shape[1])
            elif len(shape) == 4:
                ap = ap.rearrange("p (a b c) -> p a b c", a=shape[1], b=shape[2])
            elif len(shape) == 5:
                ap = ap.rearrange("p (a b c d) -> p a b c d", a=shape[1], b=shape[2], c=shape[3])
            return ap

        mask_sb = carve("attention", [HALF, 2, CTX])
        k_raw = carve("attention", [128, 2, CTX])
        k_hi = carve("attention", [128, 2, CTX], BF16)
        k_lo = carve("attention", [128, 2, CTX], BF16)
        v_raw = carve("attention", [TC, 2, NCH, D])
        v_hi = carve("attention", [TC, 2, NCH, D + 1], BF16)
        v_lo = carve("attention", [TC, 2, NCH, D], BF16)
        q_rows = carve("attention", [HALF, 2, REP, 2, D])
        q_t = carve("attention", [128, 2, REP * HALF], BF16)
        s_sb = carve("attention", [HALF, 4, CTX])
        row_max = carve("attention", [HALF, 4, 1])
        p_sb = carve("attention", [TC, 4, NCH * HALF])
        p_lo = carve("attention", [TC, 4, NCH * HALF], BF16)
        r_den = carve("attention", [HALF, 2, REP])

        w1_hi = carve("ffn", [128, KC, F1], BF16)
        w1_lo = carve("ffn", [128, KC, F1], BF16)
        wq_cat = carve("ffn", [128, KC, 2 * BOT], BF16)
        h_rows = carve("ffn", [HALF, 2, 2 * GW])
        h_hi = carve("ffn", [128, 4, 4, HALF], BF16)
        h_lo = carve("ffn", [128, 4, 4, HALF], BF16)
        keys_aug = carve("ffn", [128, NSLOT])
        rk_aug = carve("ffn", [128, NSLOT])
        v2 = carve("ffn", [128, 4, VB])
        b1_rows = carve("ffn", [HALF, F1])
        w2_rows = carve("ffn", [HALF, F1])
        stage_at = used["ffn"]
        z_all = carve("ffn", [128, 2 * BATCH * HALF])
        w_rows = carve("ffn", [HALF, NSLOT])
        w_t = carve("ffn", [128, 4, HALF])
        logits = carve("ffn", [HALF, NSLOT])
        unsel = carve("ffn", [HALF, NSLOT])
        used["ffn"] = stage_at + STAGE_SLOTS * (2 * NSLOT + 2 * VB)
        q_aug = carve("ffn", [128, HALF])
        rq_aug = carve("ffn", [128, HALF])
        q_tmp = carve("ffn", [64, HALF])
        g_rows = carve("ffn", [HALF, F1])
        wvu = arena[:, 0:HID]
        z_cur = arena[:, HID:HID + 2 * HALF].rearrange("p (h c) -> p h c", h=2)

        assert used["attention"] <= stage_at
        stage = arena[:, stage_at:stage_at + 2 * 4 * F1].rearrange("p (s k n) -> p s k n", s=2, k=4)
        slots = arena[:, stage_at:stage_at + STAGE_SLOTS * (2 * NSLOT + 2 * VB)].rearrange("p (s n) -> p s n", s=STAGE_SLOTS)
        av_stage = slots[:, :, 0:2 * NSLOT].rearrange("p s (k n) -> p s k n", k=2)
        wvd_stage = slots[:, :, 2 * NSLOT:2 * NSLOT + 2 * VB].rearrange("p s (k n) -> p s k n", k=2)
        wq_raw = arena[:, 9216:9216 + KC * BOT].rearrange("p (k n) -> p k n", k=KC)
        wr_t = sb("wr_t", [128, RDIM])
        scal = sb("scal", [HALF, 4])
        tanh_gf = sb("tanh_gf", [HALF, 1])
        ones = stats[:, :, :, :].rearrange("p h a n -> p (h a n)")[:, 0:HALF]
        bn2 = sb("bn2", [HALF, 4, 6])
        mv2 = sb("mv2", [HALF, 2])
        ve2 = sb("ve2", [HALF, 1])
        half2 = sb("half2", [HALF, 1])
        rs2 = sb("rs2", [HALF, 1])
        top8 = sb("top8", [HALF, 8])
        neg_top = sb("neg_top", [HALF, 1])
        w_sum = sb("w_sum", [HALF, 1])
        dot = sb("dot", [HALF, 1])
        mean_all = sb("mean_all", [HALF, FFN_TILES])
        var_all = sb("var_all", [HALF, FFN_TILES])
        rstd_all = sb("rstd_all", [HALF, FFN_TILES])
        wsum_all = sb("wsum_all", [HALF, FFN_TILES])
        learned = sb("learned", [HALF, FFN_TILES])
        gate = sb("gate", [HALF, 12, FFN_TILES])

        psum = pb("psum", [128, 8, 512])
        score_ps = psum[:, 0:4, :].rearrange("p (s c) n -> p s c n", s=2)
        tr_ps = psum[:, 4:6, :]
        mix_ps = psum[:, 6:8, :]

        consts_set = sem("consts_set")
        ident_ready = sem("ident_ready")
        paddings_set = sem("paddings_set")
        gx_loaded = sem("gx_loaded")
        gx_tanh = sem("gx_tanh")
        x_first = [sem(f"x_first{i}") for i in range(PAIRS_A_BATCH)]
        x_next = sem("x_next")
        mask_loaded = sem("mask_loaded")
        norm_summed = sem("norm_summed")
        meanvar_done = sem("meanvar_done")
        window_copied = sem("window_copied")
        rstd_done = sem("rstd_done")
        veps_done = sem("veps_done")
        norm_set = sem("norm_set")
        k_loaded = [sem("k_loaded0"), sem("k_loaded1")]
        v_loaded = [sem("v_loaded0"), sem("v_loaded1")]
        k_hi_done = sem("k_hi_done")
        k_split = sem("k_split")
        v_hi_done = sem("v_hi_done")
        v_split = sem("v_split")
        q_staged = sem("q_staged")
        q_turned = sem("q_turned")
        q_hi_done = sem("q_hi_done")
        q_split = sem("q_split")
        scored = sem("scored")
        wait_over = sem("wait_over")
        maxed = sem("maxed")
        shifted_v = sem("shifted_v")
        shifted_a = sem("shifted_a")
        turned = sem("turned")
        exped = sem("exped")
        p_split = sem("p_split")
        mixed = sem("mixed")
        den_done = sem("den_done")
        x_added = sem("x_added")
        out_stored = sem("out_stored")

        stage_loaded = [sem("stage_loaded0"), sem("stage_loaded1")]
        weights_loaded = sem("weights_loaded")
        rows_loaded = sem("rows_loaded")
        rel_loaded = sem("rel_loaded")
        v2_loaded = [sem(f"v2_loaded{i}") for i in range(STAGE_SLOTS)]
        v2_ready = sem("v2_ready")
        preact_done = sem("preact_done")
        dotted = sem("dotted")
        small_loaded = sem("small_loaded")
        pads_set = sem("pads_set")
        v2_piece = sem("v2_piece")
        w1_hi_done = sem("w1_hi_done")
        w1_split = sem("w1_split")
        wq_hi_done = sem("wq_hi_done")
        wq_split = sem("wq_split")
        rk_summed = sem("rk_summed")
        tables_ready = sem("tables_ready")
        bn2_done = sem("bn2_done")
        mv2_done = sem("mv2_done")
        ve2_done = sem("ve2_done")
        rs2_done = sem("rs2_done")
        logits_done = sem("logits_done")
        gate_inner = sem("gate_inner")
        h_staged = sem("h_staged")
        h_turned = sem("h_turned")
        h_hi_done = sem("h_hi_done")
        h_split = sem("h_split")
        quarter_summed = sem("quarter_summed")
        q_half = sem("q_half")
        q_ready = sem("q_ready")
        rq_summed = sem("rq_summed")
        rq_ready = sem("rq_ready")
        routed = sem("routed")
        topped = sem("topped")
        selected = sem("selected")
        weighed = sem("weighed")
        w_turned = sem("w_turned")
        w_t_ready = sem("w_t_ready")
        z_summed = sem("z_summed")
        z_ready = sem("z_ready")
        gelu_done = sem("gelu_done")
        ones_set = sem("ones_set")
        wvu_loaded = sem("wvu_loaded")
        gf_tanh = sem("gf_tanh")
        log_var_done = sem("log_var_done")
        mean_summed = sem("mean_summed")
        gate_v = sem("gate_v")
        gate_a = sem("gate_a")
        z_copied = sem("z_copied")
        aux_summed = sem("aux_summed")
        base_done = sem("base_done")
        y_done = sem("y_done")

        block = ctx.enter_context(nc.Block())

        def shifts_on_act(k):
            return k % 2 == 1

        def sweep(eng, step, ahead=None):
            for k in range(-8, 0):
                step(0, k, False)
            parts = ((0, PAIRS - 1),) if ahead is None else ((0, PAIRS - PAIRS_A_BATCH), (PAIRS - PAIRS_A_BATCH, PAIRS - 1))
            for first, end in parts:
                with eng.Fori(first, end) as pair:
                    for k in range(PER_PAIR):
                        if ahead is not None and end == PAIRS - PAIRS_A_BATCH:
                            ahead(pair, k)
                        step(pair, k, False)
            for k in range(PER_PAIR + 2):
                step(PAIRS - 1, k, True)

        def sweep_tiles(eng, step):
            for i in (-1, 0, 1):
                step(0, i)
            with eng.Fori(1, BATCH - 1) as b:
                for i in range(2):
                    step(b, i)
            for i in range(4):
                step(BATCH - 1, i)

        def in_range(b, i):
            return not isinstance(b, int) or 0 <= 2 * b + i < FFN_TILES

        def from_tile(b, i, first):
            return not isinstance(b, int) or 2 * b + i >= first

        def rows_of(b, i):
            flat = x_sb[:, bass.ds(b * (2 * HID) + i // 2 * (2 * HID), 2 * HID)]
            return flat.rearrange("p (g h c) -> p g h c", g=KV, h=2)[:, :, i % 2, :]

        def count(pair, per_pair, local):
            return pair * per_pair + local

        def pair_of_x(pair):
            return x_sb[:, bass.ds(pair * (4 * GW), 4 * GW)]

        def x_rows(pair):
            return x[bass.ds(pair, 1)].rearrange("o p n -> (o p) n")

        @block.sync
        def _(sp):
            for i in (0, 2):
                sp.dma_start(pair_of_x(i), x_rows(i)).then_inc(x_first[i], 16)

            def load(pair, u):
                g = count(pair, 2, u)
                for part in range(2):
                    sp.dma_start(k_raw[D * part:D * part + D, u, :], k_t[bass.ds(g, 1)].rearrange("o d t -> (o d) t")).then_inc(k_loaded[u], 16)
                sp.dma_start(v_raw[:, u], v_rows[bass.ds(g, 1)].rearrange("o p (c d) -> (o p) c d", c=NCH)).then_inc(v_loaded[u], 16)

            load(0, 0)
            load(0, 1)
            sp.dma_start(pair_of_x(PAIRS_A_BATCH), x_rows(PAIRS_A_BATCH)).then_inc(x_next, 16)
            for i in range(2):
                sp.dma_start(stage[:, i], w1_t[i]).then_inc(stage_loaded[i], 16)
            for dst, src in ((wr_t[0:BOT], wr), (scal, scalars)):
                sp.dma_start(dst[:], src).then_inc(small_loaded, 16)
            for first, end in ((1, PAIRS - PAIRS_A_BATCH), (PAIRS - PAIRS_A_BATCH, PAIRS)):
                with sp.Fori(first, end) as pair:
                    if end < PAIRS:
                        sp.wait_ge(x_next, count(pair, 16, 0))
                        sp.dma_start(pair_of_x(pair + PAIRS_A_BATCH), x_rows(pair + PAIRS_A_BATCH)).then_inc(x_next, 16)
                    for u in range(2):
                        sp.wait_ge(k_split, count(pair, 2, u - 1))
                        sp.wait_ge(v_split, count(pair, 2, u - 1))
                        load(pair, u)
            sp.wait_ge(x_added, NHALF)
            sp.dma_start(keys_aug[0:BOT, :], keys_t).then_inc(weights_loaded, 16)
            sp.dma_start(wq_raw, wq_t).then_inc(weights_loaded, 16)
            sp.dma_start(b1_rows, b1).then_inc(rows_loaded, 16)
            sp.dma_start(w2_rows, w2).then_inc(rows_loaded, 16)
            for i in range(2, 4):
                sp.wait_ge(w1_split, i - 1)
                sp.dma_start(stage[:, i % 2], w1_t[i]).then_inc(stage_loaded[i % 2], 16)
            sp.wait_ge(pads_set, 1)
            sp.dma_start(keys_aug[BOT:BOT + 1, :], log_rel).then_inc(rel_loaded, 16)
            sp.dma_start(rk_aug[BOT:BOT + 1, :], log_rel).then_inc(rel_loaded, 16)
            sp.wait_ge(w1_split, 4)
            for i in range(KC // 2):
                if i >= STAGE_SLOTS:
                    sp.wait_ge(v2_piece, i - STAGE_SLOTS + 1)
                slot = i % STAGE_SLOTS
                sp.dma_start(av_stage[:, slot], av_t[i]).then_inc(v2_loaded[slot], 16)
                sp.dma_start(wvd_stage[:, slot], wvd_t[i]).then_inc(v2_loaded[slot], 16)
            sp.wait_ge(quarter_summed, 4 * FFN_TILES)
            sp.dma_start(wvu, wvu_t).then_inc(wvu_loaded, 16)
            with sp.Fori(0, BATCH) as b:
                sp.wait_ge(y_done, b * 2 + 2)
                sp.dma_start(out[bass.ds(b, 1)].rearrange("o p g h c -> (o p) (g h c)"),
                             x_sb[:, bass.ds(b * (2 * HID), 2 * HID)]).then_inc(out_stored, 16)
            sp.wait_ge(out_stored, 16 * BATCH)

        @block.gpsimd
        def _(pool):
            pool.memset(ident[:, :], 0.0).then_inc(consts_set, 1)
            pool.wait_ge(consts_set, 1)
            pool.affine_select(out=ident[:, :], in_=ident[:, :], compare_op=ALU.not_equal, fill=1.0,
                               base=0, pattern=[[-1, 128]], channel_multiplier=1).then_inc(ident_ready, 1)
            pool.memset(minus_half[:, :], -0.5).then_inc(consts_set, 1)
            pool.wait_ge(consts_set, 2)

            def root(pair):
                pool.wait_ge(veps_done, count(pair, 1, 2))
                pool.tensor_tensor(rstd[:, :], veps[:, :], minus_half[:, :], ALU.pow).then_inc(rstd_done, 1)

            root(-1)

            def step(pair, k, last):
                n = k + 2
                if n >= 0 and not (last and n >= PER_PAIR):
                    pool.wait_ge(exped, count(pair, 16, n + 1))
                    pool.tensor_tensor(p_lo[:, n % 4, :], p_sb[:, n % 4, :], high(p_sb[:, n % 4, :]),
                                       ALU.subtract).then_inc(p_split, 1)
                if k in (-7, 2, 10):
                    g = (k + 7) // 8 if k > 0 else 0
                    if not (last and g >= 2):
                        pool.wait_ge(v_hi_done, count(pair, 2, g + 1))
                        pool.tensor_tensor(v_lo[:, g % 2], v_raw[:, g % 2], v_hi[:, g % 2, :, 0:D],
                                           ALU.subtract).then_inc(v_split, 1)

            sweep(pool, step, lambda pair, k: root(pair) if k == 7 else None)

            pool.memset(half2[:, :], -0.5).then_inc(consts_set, 1)
            pool.memset(ones[:, :], 1.0).then_inc(ones_set, 1)
            pool.wait_ge(consts_set, 3)

            def norm(b, i):
                if in_range(b, i + 1):
                    pool.wait_ge(ve2_done, count(b, 2, i + 2))
                    if from_tile(b, i, 0):
                        pool.wait_ge(h_staged, count(b, 8, 4 * i + 4))
                    pool.tensor_tensor(rs2[:, :], ve2[:, :], half2[:, :], ALU.pow).then_inc(rs2_done, 1)

            sweep_tiles(pool, norm)

        @block.scalar
        def _(act):
            act.dma_start(tanh_gx[:, :], g_x).then_inc(gx_loaded, 16)
            for i in (1, 3):
                act.dma_start(pair_of_x(i), x_rows(i)).then_inc(x_first[i], 16)
            act.dma_start(mask_sb[:, :, :], mask).then_inc(mask_loaded, 16)
            act.wait_ge(gx_loaded, 16)
            act.activation(tanh_gx[:, :], tanh_gx[:, :], ACT.Tanh).then_inc(gx_tanh, 1)

            def step(pair, k, last):
                h = {-7: 0, -3: 1}.get(k, (k - 2) // 4 + 2 if k >= 0 and k % 4 == 3 else None)
                if h is not None and not (last and h >= 4):
                    act.wait_ge(q_turned, count(pair, 4, h + 1))
                    act.activation(q_t[:, h % 2, :], mix_ps[:, (h + 1) % 2, 0:REP * HALF], ACT.Copy).then_inc(q_hi_done, 1)
                if k in (-8, 1, 9):
                    g = (k + 7) // 8 if k > 0 else 0
                    if not (last and g >= 2):
                        u = g % 2
                        act.wait_ge(k_loaded[u], count(pair, 32, 32 * (g // 2 + 1)))
                        if k > 0:
                            act.wait_ge(scored, count(pair, 16, 8 * g - 8))
                        act.activation(k_hi[:, u, :], k_raw[:, u, :], ACT.Copy).then_inc(k_hi_done, 1)
                        act.wait_ge(v_loaded[u], count(pair, 16, 16 * (g // 2 + 1)))
                        if k > 0:
                            act.wait_ge(mixed, count(pair, 4, 2 * g - 2))
                        if k < 0:
                            act.wait_ge(paddings_set, 1)
                        act.activation(v_hi[:, u, :, 0:D], v_raw[:, u], ACT.Copy).then_inc(v_hi_done, 1)
                n = k + 3
                if shifts_on_act(n) and n >= 0 and not (last and n >= PER_PAIR):
                    act.wait_ge(maxed, count(pair, 16, n + 1))
                    act.activation(s_sb[:, n % 4, :], s_sb[:, n % 4, :], ACT.Identity, bias=row_max[:, n % 4, :],
                                   scale=-1.0).then_inc(shifted_a, 1)
                n = k + 2
                if n >= 0 and not (last and n >= PER_PAIR):
                    act.wait_ge(turned, count(pair, 16, n + 1))
                    act.activation(p_sb[:, n % 4, :].rearrange("p (a c) -> p a c", a=2),
                                   tr_ps[0:TC, :, 0:NCH // 2 * HALF], ACT.Exp,
                                   scale=-1.0 if shifts_on_act(n) else 1.0).then_inc(exped, 1)

            sweep(act, step)

            act.wait_ge(x_added, NHALF)
            for i in range(4):
                act.wait_ge(stage_loaded[i % 2], 16 * (1 + i // 2))
                act.activation(w1_hi[:, 4 * i:4 * i + 4, :], stage[:, i % 2], ACT.Copy).then_inc(w1_hi_done, 1)
                if i == 1:
                    act.wait_ge(weights_loaded, 32)
                    act.activation(wq_cat[:, :, 0:BOT], wq_raw, ACT.Copy).then_inc(wq_hi_done, 1)
                    act.wait_ge(rk_summed, 1)
                    act.wait_ge(pads_set, 1)
                    act.activation(keys_aug[0:BOT, :], keys_aug[0:BOT, :], ACT.Copy, scale=float(BOT) ** -0.5).then_inc(tables_ready, 1)
                    act.activation(rk_aug[0:RDIM, :], psum[0:RDIM, 5, :], ACT.Copy, scale=float(RDIM) ** -0.5).then_inc(tables_ready, 1)

            def ffn(b, i):
                for j in range(4):
                    if in_range(b, i + 1):
                        act.wait_ge(h_turned, count(b, 8, 4 * (i + 1) + j + 1))
                        if from_tile(b, i, 0):
                            act.wait_ge(quarter_summed, count(b, 8, 4 * i + j + 1))
                        act.activation(h_hi[:, j], psum[:, j % 2, 0:4 * HALF].rearrange("p (k n) -> p k n", k=4),
                                       ACT.Copy).then_inc(h_hi_done, 1)
                    if in_range(b, i - 1) and j == 0:
                        act.wait_ge(rq_summed, count(b, 2, i))
                        act.activation(rq_aug[0:RDIM, :], psum[0:RDIM, 5, 0:HALF], ACT.Copy).then_inc(rq_ready, 1)
                    if in_range(b, i - 2) and j == 1:
                        act.wait_ge(z_summed, count(b, 2, i - 1))
                        act.activation(z_all[:, bass.ds(b * (2 * HALF) + (i - 2) * HALF, HALF)],
                                       psum[:, 6, 0:HALF], ACT.Copy).then_inc(z_ready, 1)
                    if isinstance(b, int) and 2 * b + i == 1 and j == 1:
                        act.wait_ge(v2_piece, KC // 2)
                        act.activation(v2, psum[:, 6, :].rearrange("p (m n) -> p m n", m=4), ACT.Copy).then_inc(v2_ready, 1)
                    if in_range(b, i - 1) and j == 3:
                        act.wait_ge(selected, count(b, 2, i))
                        act.activation(w_rows, logits, ACT.Exp, bias=neg_top[:, :], accum_out=w_sum[:, :]).then_inc(weighed, 1)
                        act.wait_ge(w_turned, count(b, 2, i))
                        act.activation(w_t, psum[:, 6, 0:4 * HALF].rearrange("p (m n) -> p m n", m=4), ACT.Copy).then_inc(w_t_ready, 1)
                if in_range(b, i):
                    act.wait_ge(quarter_summed, count(b, 8, 4 * i + 4))
                    act.activation(q_tmp, psum[BOT:2 * BOT, 3, 0:HALF], ACT.Copy).then_inc(q_half, 1)
                    act.wait_ge(preact_done, count(b, 2, i + 1))
                    act.activation(g_rows, g_rows, ACT.Gelu_apprx_tanh).then_inc(gelu_done, 1)

            act.wait_ge(small_loaded, 32)
            sweep_tiles(act, ffn)

            act.activation(tanh_gf[:, :], scal[:, 0:1], ACT.Tanh).then_inc(gf_tanh, 1)
            act.wait_ge(gate_v, 1)
            act.activation(gate[:, 1, :], gate[:, 0, :], ACT.Ln, bias=1.0).then_inc(log_var_done, 1)
            act.wait_ge(gate_v, 3)
            act.activation(gate[:, 3, :], gate[:, 2, :], ACT.Exp, scale=-1.0).then_inc(gate_a, 1)
            act.wait_ge(gate_v, GATE_EXP)
            act.activation(gate[:, 3, :], gate[:, 2, :], ACT.Exp, scale=-1.0).then_inc(gate_a, 1)
            act.wait_ge(gate_v, GATE_BASE)

            def base(b, i):
                at = count(b, 2 * HALF, i * HALF)
                if not isinstance(b, int) or b > 0:
                    act.wait_ge(aux_summed, b * 2 + i - 1)
                act.activation(z_cur[:, i, :], z_all[:, bass.ds(at, HALF)], ACT.Copy).then_inc(z_copied, 1)
                act.activation(rows_of(b, i), rows_of(b, i), ACT.Identity, bias=gate[:, 9, bass.ds(b * 2 + i, 1)],
                               scale=gate[:, 8, bass.ds(b * 2 + i, 1)]).then_inc(base_done, 1)

            for i in range(2):
                base(0, i)
            with act.Fori(1, BATCH) as b:
                for i in range(2):
                    base(b, i)

        @block.tensor
        def _(pe):
            pe.wait_ge(ident_ready, 1)

            def turn_q(pair, h):
                pe.wait_ge(q_staged, count(pair, 4, h + 1))
                if not isinstance(pair, int) or 4 * pair + h >= 3:
                    pe.wait_ge(x_added, count(pair, 4, h - 2))
                for r in range(REP):
                    mm = pe.transpose(mix_ps[:, (h + 1) % 2, r * HALF:(r + 1) * HALF],
                                      q_rows[:, h % 2, r].rearrange("p a d -> p (a d)"), ident[0:HALF, 0:HALF])
                mm.then_inc(q_turned, 1)

            def score(pair, n):
                h, u = n // 4, n // 8 % 2
                if n % 8 == 0:
                    pe.wait_ge(k_split, count(pair, 2, n // 8 + 1))
                if n % 4 == 0:
                    pe.wait_ge(q_split, count(pair, 4, h + 1))
                if not isinstance(pair, int) or n >= 2:
                    pe.wait_ge(maxed, count(pair, 16, n - 1))
                q = q_t[:, h % 2, (n % 4) * HALF:(n % 4 + 1) * HALF]
                for i, part in enumerate((k_hi, k_lo)):
                    for c in range(2):
                        mm = pe.matmul(score_ps[0:HALF, n % 2, c, 0:CTX // 2], q,
                                       part[:, u, c * (CTX // 2):(c + 1) * (CTX // 2)], start=(i == 0), stop=(i == 1))
                mm.then_inc(scored, 1)

            def turn(pair, n):
                if shifts_on_act(n):
                    pe.wait_ge(shifted_a, count(pair, 8, n // 2 + 1))
                else:
                    pe.wait_ge(shifted_v, count(pair, 8, n // 2 + 1))
                if not isinstance(pair, int) or n >= 1:
                    pe.wait_ge(exped, count(pair, 16, n))
                for c in range(NCH):
                    at = c % 3 * HALF
                    mm = pe.transpose(tr_ps[0:TC, c // 3, at:at + HALF], s_sb[:, n % 4, c * TC:(c + 1) * TC],
                                      ident[0:HALF, 0:HALF])
                mm.then_inc(turned, 1)

            def mix(pair, n, last):
                h, u = n // 4, n // 8 % 2
                if n % 8 == 0:
                    pe.wait_ge(v_split, count(pair, 2, n // 8 + 1))
                if n % 4 == 0 and not (last and h + 1 >= 4):
                    pe.wait_ge(q_split, count(pair, 4, h + 2))
                pe.wait_ge(p_split, count(pair, 16, n + 1))
                at = n % 4 * (D + 1)
                for c in range(NCH):
                    hi = high(p_sb[:, n % 4, c * HALF:(c + 1) * HALF])
                    lo = p_lo[:, n % 4, c * HALF:(c + 1) * HALF]
                    pe.matmul(mix_ps[0:HALF, h % 2, at:at + D + 1], hi, v_hi[:, u, c, :],
                              start=(c == 0), stop=False, skip_group_check=True)
                    pe.matmul(mix_ps[0:HALF, h % 2, at:at + D], hi, v_lo[:, u, c, :],
                              start=False, stop=False, skip_group_check=True)
                    mm = pe.matmul(mix_ps[0:HALF, h % 2, at:at + D + 1], lo, v_hi[:, u, c, :],
                                   start=False, stop=(c == NCH - 1), skip_group_check=True)
                if n % 4 == 3:
                    mm.then_inc(mixed, 1)

            def step(pair, k, last):
                n = k + 4
                if n >= 0 and not (last and n >= PER_PAIR):
                    score(pair, n)
                h = {-7: 0, -6: 1}.get(k, k // 4 + 2 if k >= 0 and k % 4 == 2 else None)
                if h is not None and not (last and h >= 4):
                    turn_q(pair, h)
                n = k + 2
                if n >= 0 and not (last and n >= PER_PAIR):
                    turn(pair, n)
                if k >= 0 and not (last and k >= PER_PAIR):
                    mix(pair, k, last)

            sweep(pe, step)

            pe.wait_ge(x_added, NHALF)
            pe.wait_ge(weights_loaded, 32)
            pe.wait_ge(small_loaded, 32)
            pe.matmul(psum[0:RDIM, 5, :], wr_t[0:BOT, :], keys_aug[0:BOT, :], start=True, stop=True).then_inc(rk_summed, 1)
            def sum_v2(pieces):
                for i in pieces:
                    pe.wait_ge(v2_loaded[i % STAGE_SLOTS], 32 * (1 + i // STAGE_SLOTS))
                    for kk in range(2):
                        for m in range(4):
                            mm = pe.matmul(psum[:, 6, m * 128:(m + 1) * 128], av_stage[:, i % STAGE_SLOTS, kk, m * 128:(m + 1) * 128],
                                           wvd_stage[:, i % STAGE_SLOTS, kk, :], start=(i == 0 and kk == 0 and m == 0),
                                           stop=(i == KC // 2 - 1 and kk == 1), skip_group_check=True)
                    mm.then_inc(v2_piece, 1)

            def turn_h(b, i, j):
                pe.wait_ge(h_staged, count(b, 8, 4 * i + j + 1))
                if from_tile(b, i, 1) or j >= 2:
                    pe.wait_ge(h_split, count(b, 8, 4 * i + j - 1))
                for k in range(4):
                    mm = pe.transpose(psum[:, j % 2, k * HALF:(k + 1) * HALF],
                                      h_rows[:, j % 2, k * 128:(k + 1) * 128], ident[0:HALF, 0:HALF])
                mm.then_inc(h_turned, 1)

            def sum_quarter(b, i, j):
                pe.wait_ge(h_split, count(b, 8, 4 * i + j + 1))
                if isinstance(b, int) and 2 * b + i == 0:
                    pe.wait_ge(w1_split, j + 1)
                if j == 0 and from_tile(b, i, 2):
                    pe.wait_ge(preact_done, count(b, 2, i - 1))
                for kk in range(4):
                    k = 4 * j + kk
                    for n, (h, w) in enumerate(((h_hi, w1_hi), (h_hi, w1_lo), (h_lo, w1_hi))):
                        pe.matmul(psum[0:HALF, 2 if i % 2 == 0 else 7, :], h[:, j, kk, :], w[:, k, :],
                                  start=(k == 0 and n == 0), stop=(k == KC - 1 and n == 2))
                if isinstance(b, int) and 2 * b + i == 0 and j == 0:
                    pe.wait_ge(wq_split, 1)
                if j == 0 and from_tile(b, i, 1):
                    pe.wait_ge(q_ready, count(b, 2, i))
                for kk in range(4):
                    k = 4 * j + kk
                    for n, h in enumerate((h_hi, h_lo)):
                        mm = pe.matmul(psum[:, 3, 0:HALF], wq_cat[:, k, :], h[:, j, kk, :], start=(k == 0 and n == 0),
                                       stop=(k == KC - 1 and n == 1))
                mm.then_inc(quarter_summed, 1)

            def ffn(b, i):
                for j in range(4):
                    if in_range(b, i):
                        sum_quarter(b, i, j)
                    if in_range(b, i + 1):
                        turn_h(b, i + 1, j)
                    if isinstance(b, int) and (2 * b + i, j) in V2_TURNS:
                        sum_v2(V2_TURNS[2 * b + i, j])
                    if in_range(b, i - 1) and j == 0:
                        pe.wait_ge(q_ready, count(b, 2, i))
                        if from_tile(b, i, 2):
                            pe.wait_ge(selected, count(b, 2, i - 1))
                        pe.matmul(psum[0:RDIM, 5, 0:HALF], wr_t[:, :], q_aug, start=True, stop=True).then_inc(rq_summed, 1)
                    if in_range(b, i - 2) and j == 0:
                        pe.wait_ge(w_t_ready, count(b, 2, i - 1))
                        if isinstance(b, int):
                            pe.wait_ge(v2_ready, 1)
                        for m in range(4):
                            mm = pe.matmul(psum[:, 6, 0:HALF], v2[:, m, :], w_t[:, m, :], start=(m == 0), stop=(m == 3))
                        mm.then_inc(z_summed, 1)
                    if in_range(b, i - 1) and j == 1:
                        pe.wait_ge(rq_ready, count(b, 2, i))
                        if isinstance(b, int) and 2 * b + i == 1:
                            pe.wait_ge(tables_ready, 2)
                            pe.wait_ge(rel_loaded, 32)
                        pe.matmul(psum[0:HALF, 4, :], rq_aug, rk_aug, start=True, stop=True)
                        pe.matmul(psum[0:HALF, 5, :], q_aug, keys_aug, start=True, stop=True).then_inc(routed, 1)
                    if in_range(b, i - 1) and j == 3:
                        pe.wait_ge(weighed, count(b, 2, i))
                        if isinstance(b, int) and 2 * b + i == 1:
                            pe.wait_ge(v2_ready, 1)
                        if from_tile(b, i, 2):
                            pe.wait_ge(z_ready, count(b, 2, i - 1))
                        for m in range(4):
                            mm = pe.transpose(psum[:, 6, m * HALF:(m + 1) * HALF], w_rows[:, m * 128:(m + 1) * 128],
                                              ident[0:HALF, 0:HALF])
                        mm.then_inc(w_turned, 1)

            pe.wait_ge(paddings_set, 2)
            sweep_tiles(pe, ffn)

            pe.wait_ge(gate_v, 2)
            pe.wait_ge(ones_set, 1)
            pe.matmul(psum[0:HALF, 0, 0:1], ones[:, :], gate[:, 2, 0:1], start=True, stop=True).then_inc(mean_summed, 1)
            pe.wait_ge(gate_v, GATE_BASE)
            pe.wait_ge(wvu_loaded, 16)

            def aux(b, i):
                pe.wait_ge(z_copied, b * 2 + i + 1)
                if not isinstance(b, int) or b > 0:
                    pe.wait_ge(y_done, b * 2 + i - 1)
                for n in range(4):
                    mm = pe.matmul(psum[0:HALF, 4 * i + n, :], z_cur[:, i, :], wvu[:, n * 512:(n + 1) * 512], start=True, stop=True)
                mm.then_inc(aux_summed, 1)

            for i in range(2):
                aux(0, i)
            with pe.Fori(1, BATCH) as b:
                for i in range(2):
                    aux(b, i)

        @block.vector
        def _(dve):
            def wait_alone(s, value):
                dve.wait_ge(s, value)
                dve.sem_inc(wait_over, 1)

            dve.memset(v_hi[:, :, :, :], 1.0).then_inc(paddings_set, 1)
            dve.memset(wr_t[BOT:128, :], 0.0).then_inc(paddings_set, 1)

            def norm_stats(pair, h):
                groups = pair_of_x(pair).rearrange("p (g h c) -> p g h c", g=2, h=2)
                dve.bn_stats(stats[:, h, bass.ds(pair, 1), :].rearrange("p o n -> p (o n)"), groups[:, :, h, :]).then_inc(norm_summed, 1)

            def norm_mean(pair):
                dve.wait_ge(norm_summed, count(pair, 2, 2 * PAIRS_A_BATCH + 2))
                dve.tensor_copy(window[:, :, :, :], stats[:, :, bass.ds(pair + 1, PAIRS_A_BATCH), :]).then_inc(window_copied, 1)
                wait_alone(window_copied, count(pair, 1, 2))
                for h in range(2):
                    dve.bn_aggr(meanvar[:, h, :], window[:, h, :, :]).then_inc(meanvar_done, 1)

            def norm_eps(pair):
                dve.wait_ge(meanvar_done, count(pair, 2, 4))
                dve.tensor_scalar(veps[:, :], meanvar[:, :, 1], EPS, None, ALU.add).then_inc(veps_done, 1)
                dve.tensor_copy(ln_mean[:, bass.ds(pair + PAIRS_A_BATCH, 1), :].rearrange("p o h -> p (o h)"), meanvar[:, :, 0]).then_inc(norm_set, 1)

            def norm_scale(pair):
                dve.wait_ge(rstd_done, count(pair, 1, 2))
                dve.tensor_scalar(ln_scale[:, bass.ds(pair + PAIRS_A_BATCH, 1), :].rearrange("p o h -> p (o h)"), rstd[:, :],
                                  float(D) ** -0.5, None, ALU.mult).then_inc(norm_set, 1)

            for i in range(PAIRS_A_BATCH):
                dve.wait_ge(x_first[i], 16)
                norm_stats(i, 0)
                norm_stats(i, 1)
            norm_mean(-1)
            norm_eps(-1)
            norm_scale(-1)
            dve.wait_ge(norm_set, 2)

            def ahead(pair, k):
                if k == 0:
                    dve.wait_ge(x_next, count(pair, 16, 16))
                    norm_stats(pair + PAIRS_A_BATCH, 0)
                elif k == 4:
                    norm_stats(pair + PAIRS_A_BATCH, 1)
                elif k == 6:
                    norm_mean(pair)
                    norm_eps(pair)
                elif k == 9:
                    norm_scale(pair)
                    dve.wait_ge(norm_set, count(pair, 2, 4))

            dve.wait_ge(mask_loaded, 16)
            dve.wait_ge(gx_tanh, 1)

            def stage_q(pair, h):
                if not isinstance(pair, int) or h >= 2:
                    dve.wait_ge(q_turned, count(pair, 4, h - 1))
                slot = (pair + h // 4) // PAIRS_A_BATCH * PAIRS_A_BATCH + PAIRS_A_BATCH - 1
                at = count(pair, 4 * GW, h * GW)
                mcol = ln_mean[:, :, :].rearrange("p a h -> p (a h)")[:, bass.ds(slot * 2 + h % 2, 1)]
                scol = ln_scale[:, :, :].rearrange("p a h -> p (a h)")[:, bass.ds(slot * 2 + h % 2, 1)]
                dve.tensor_scalar(q_rows[:, h % 2], x_sb[:, bass.ds(at, GW)].rearrange("p (r d) -> p r d", r=REP).unsqueeze(2).broadcast_to([HALF, REP, 2, D]),
                                  mcol, scol, ALU.subtract, ALU.mult).then_inc(q_staged, 1)

            def add_mix(pair, h):
                o = mix_ps[0:HALF, h % 2, 0:REP * (D + 1)].rearrange("p (r e) -> p r e", r=REP)
                dve.wait_ge(mixed, count(pair, 4, h + 1))
                dve.reciprocal(r_den[:, 0, :], o[:, :, D]).then_inc(den_done, 1)
                dve.wait_ge(den_done, count(pair, 8, 2 * h + 1))
                dve.tensor_scalar(r_den[:, 1, :], r_den[:, 0, :], tanh_gx[:, 0:1], None, ALU.mult).then_inc(den_done, 1)
                dve.wait_ge(den_done, count(pair, 8, 2 * h + 2))
                for r in range(REP):
                    xs = x_sb[:, bass.ds(count(pair, 4 * GW, h * GW + r * D), D)]
                    ins = dve.scalar_tensor_tensor(xs, o[:, r, 0:D], r_den[:, 1, r:r + 1], xs, ALU.mult, ALU.add)
                ins.then_inc(x_added, 1)

            def step(pair, k, last):
                h = {-8: 0, -7: 1}.get(k, k // 4 + 2 if k >= 0 and k % 4 == 1 else None)
                if h is not None and not (last and h >= 4):
                    stage_q(pair, h)
                h = {-6: 0, -3: 1}.get(k, (k - 2) // 4 + 2 if k >= 0 and k % 4 == 3 else None)
                if h is not None and not (last and h >= 4):
                    dve.wait_ge(q_hi_done, count(pair, 4, h + 1))
                    dve.tensor_tensor(q_t[D:2 * D, h % 2, :], mix_ps[D:2 * D, (h + 1) % 2, 0:REP * HALF],
                                      q_t[D:2 * D, h % 2, :], ALU.subtract).then_inc(q_split, 1)
                if k in (-8, 2, 10):
                    g = (k + 7) // 8 if k > 0 else 0
                    if not (last and g >= 2):
                        dve.wait_ge(k_hi_done, count(pair, 2, g + 1))
                        dve.tensor_tensor(k_lo[:, g % 2, :], k_raw[:, g % 2, :], k_hi[:, g % 2, :],
                                          ALU.subtract).then_inc(k_split, 1)
                n = k + 4
                if n >= 0 and not (last and n >= PER_PAIR):
                    wait_alone(scored, count(pair, 16, n + 1))
                    dve.tensor_tensor_reduce(
                        s_sb[:, n % 4, :].rearrange("p (a c) -> p a c", a=2), score_ps[0:HALF, n % 2, :, 0:CTX // 2],
                        mask_sb[:, n // 4 % 2, :].rearrange("p (a c) -> p a c", a=2), 1.0, -3.4e38,
                        ALU.add, ALU.max, row_max[:, n % 4, :]).then_inc(maxed, 1)
                n = k + 3
                if not shifts_on_act(n) and n >= 0 and not (last and n >= PER_PAIR):
                    dve.wait_ge(maxed, count(pair, 16, n + 1))
                    dve.tensor_scalar(s_sb[:, n % 4, :], s_sb[:, n % 4, :], row_max[:, n % 4, :], None,
                                      ALU.subtract).then_inc(shifted_v, 1)
                if k >= 0 and k % 4 == 3:
                    add_mix(pair, k // 4) if not (last and k >= PER_PAIR) else None

            sweep(dve, step, ahead)

            dve.wait_ge(x_added, NHALF)
            dve.memset(keys_aug[BOT:128, :], 0.0)
            dve.memset(rk_aug[:, :], 0.0).then_inc(pads_set, 1)

            def split_w1(i):
                dve.wait_ge(w1_hi_done, i + 1)
                dve.tensor_tensor(w1_lo[:, 4 * i:4 * i + 4, :], stage[:, i % 2], w1_hi[:, 4 * i:4 * i + 4, :],
                                  ALU.subtract).then_inc(w1_split, 1)

            def stats_of(b, i):
                rows = rows_of(b, i)
                for c in range(4):
                    ins = dve.bn_stats(bn2[:, c, :], rows[:, 2 * c:2 * c + 2, :])
                ins.then_inc(bn2_done, 1)
                wait_alone(bn2_done, count(b, 2, i + 1))
                dve.bn_aggr(mv2[:, :], bn2[:, :, :]).then_inc(mv2_done, 1)
                dve.wait_ge(mv2_done, count(b, 2, i + 1))
                dve.tensor_scalar(ve2[:, :], mv2[:, 1:2], EPS, None, ALU.add).then_inc(ve2_done, 1)
                dve.tensor_copy(mean_all[:, bass.ds(b * 2 + i, 1)], mv2[:, 0:1])
                dve.tensor_copy(var_all[:, bass.ds(b * 2 + i, 1)], mv2[:, 1:2])
                dve.wait_ge(rs2_done, count(b, 2, i + 1))
                dve.tensor_copy(rstd_all[:, bass.ds(b * 2 + i, 1)], rs2[:, :])

            def stage_h(b, i, j):
                rows = rows_of(b, i)
                if from_tile(b, i, 1) or j >= 2:
                    dve.wait_ge(h_turned, count(b, 8, 4 * i + j - 1))
                dve.tensor_scalar(h_rows[:, j % 2, :].rearrange("p (g c) -> p g c", g=2), rows[:, 2 * j:2 * j + 2, :],
                                  mv2[:, 0:1], rs2[:, :], ALU.subtract, ALU.mult).then_inc(h_staged, 1)

            def ffn(b, i):
                first = isinstance(b, int) and i < 0
                if first:
                    stats_of(b, 0)
                    split_w1(0)
                    split_w1(1)
                    dve.wait_ge(wq_hi_done, 1)
                    dve.tensor_tensor(wq_cat[:, :, BOT:2 * BOT], wq_raw, wq_cat[:, :, 0:BOT], ALU.subtract).then_inc(wq_split, 1)
                    dve.wait_ge(wq_split, 1)
                    stage_h(b, 0, 0)
                    stage_h(b, 0, 1)
                for j in range(4):
                    if in_range(b, i + 1):
                        dve.wait_ge(h_hi_done, count(b, 8, 4 * (i + 1) + j + 1))
                        dve.tensor_tensor(h_lo[:, j], psum[:, j % 2, 0:4 * HALF].rearrange("p (k n) -> p k n", k=4), h_hi[:, j],
                                          ALU.subtract).then_inc(h_split, 1)
                        if j < 2:
                            stage_h(b, i + 1, j + 2)
                    if first and j < 2:
                        split_w1(2 + j)
                    if first and j == 1:
                        dve.wait_ge(w1_split, 4)
                        dve.memset(q_aug[BOT:128, :], 0.0).then_inc(pads_set, 1)
                        dve.memset(rq_aug[:, :], 0.0).then_inc(pads_set, 1)
                        dve.wait_ge(pads_set, 3)
                        dve.memset(q_aug[BOT:BOT + 1, :], 1.0).then_inc(pads_set, 1)
                        dve.memset(rq_aug[BOT:BOT + 1, :], 1.0).then_inc(pads_set, 1)
                        dve.wait_ge(pads_set, 5)
                    if in_range(b, i + 2) and j == 1:
                        stats_of(b, i + 2)
                    if in_range(b, i + 2) and j >= 2:
                        stage_h(b, i + 2, j - 2)
                    if in_range(b, i - 1) and j == 0:
                        wait_alone(gelu_done, count(b, 2, i))
                        dve.tensor_tensor_reduce(g_rows, g_rows, w2_rows, 1.0, 0.0, ALU.mult, ALU.add, dot[:, :]).then_inc(dotted, 1)
                        dve.wait_ge(dotted, count(b, 2, i))
                        dve.tensor_copy(learned[:, bass.ds(b * 2 + i - 1, 1)], dot[:, :])
                    if in_range(b, i - 1) and j == 2:
                        router = psum[0:HALF, 4, :]
                        if isinstance(b, int) and 2 * b + i == 1:
                            dve.wait_ge(v2_piece, KC // 2)
                        wait_alone(routed, count(b, 2, i))
                        dve.max(top8[:, :], router).then_inc(topped, 1)
                        wait_alone(topped, count(b, 6, 3 * i - 2))
                        dve.match_replace(unsel, top8[:, :], router, -3.0e38).then_inc(topped, 1)
                        dve.wait_ge(topped, count(b, 6, 3 * i - 1))
                        dve.tensor_tensor(unsel, router, unsel, ALU.is_equal).then_inc(topped, 1)
                        dve.wait_ge(topped, count(b, 6, 3 * i))
                        dve.scalar_tensor_tensor(logits, unsel, -1.0e30, psum[0:HALF, 5, :], ALU.mult, ALU.add).then_inc(logits_done, 1)
                        dve.wait_ge(logits_done, count(b, 2, i))
                        dve.tensor_reduce(neg_top[:, :], logits, AX.X, ALU.max, negate=True).then_inc(selected, 1)
                    if in_range(b, i - 1) and j == 3:
                        dve.wait_ge(weighed, count(b, 2, i))
                        dve.tensor_copy(wsum_all[:, bass.ds(b * 2 + i - 1, 1)], w_sum[:, :])
                if in_range(b, i):
                    dve.wait_ge(q_half, count(b, 2, i + 1))
                    dve.tensor_tensor(q_aug[0:BOT, :], psum[0:BOT, 3, 0:HALF], q_tmp, ALU.add).then_inc(q_ready, 1)
                    if isinstance(b, int) and 2 * b + i == 0:
                        dve.wait_ge(rows_loaded, 32)
                    dve.tensor_tensor(g_rows, psum[0:HALF, 2 if i % 2 == 0 else 7, :], b1_rows, ALU.add).then_inc(preact_done, 1)

            sweep_tiles(dve, ffn)

            steps = [0]

            def gate_step(ins):
                steps[0] += 1
                ins.then_inc(gate_v, 1)
                dve.wait_ge(gate_v, steps[0])

            one = lambda n: gate[:, n, 0:1]
            dve.wait_ge(h_staged, 2 * FFN_TILES)
            dve.tensor_tensor(gate[:, 4, :], rstd_all[:, :], rstd_all[:, :], ALU.mult).then_inc(gate_inner, 1)
            dve.wait_ge(gate_inner, 1)
            gate_step(dve.tensor_tensor(gate[:, 0, :], var_all[:, :], gate[:, 4, :], ALU.mult))
            dve.wait_ge(log_var_done, 1)
            gate_step(dve.tensor_reduce(one(2), gate[:, 1, :], AX.X, ALU.add))
            dve.wait_ge(mean_summed, 1)
            dve.tensor_scalar(one(5), psum[0:HALF, 0, 0:1], 1.0 / ROWS, 1e-6, ALU.mult, ALU.add).then_inc(gate_inner, 1)
            dve.wait_ge(gate_inner, 2)
            dve.reciprocal(one(6), one(5)).then_inc(gate_inner, 1)
            gate_step(dve.tensor_scalar(gate[:, 2, :], learned[:, :], scal[:, 3:4], None, ALU.add))
            dve.wait_ge(gate_inner, 3)
            gate_step(dve.tensor_scalar(gate[:, 7, :], gate[:, 1, :], one(6), 0.5, ALU.mult, ALU.mult))
            dve.wait_ge(gate_a, 1)
            gate_step(dve.tensor_scalar(gate[:, 4, :], gate[:, 3, :], 1.0, None, ALU.add))
            gate_step(dve.reciprocal(gate[:, 5, :], gate[:, 4, :]))
            gate_step(dve.scalar_tensor_tensor(gate[:, 4, :], gate[:, 5, :], 2.5, gate[:, 7, :], ALU.mult, ALU.add))
            gate_step(dve.tensor_scalar(gate[:, 5, :], gate[:, 4, :], 0.0, 5.0, ALU.max, ALU.min))
            gate_step(dve.tensor_scalar(gate[:, 4, :], gate[:, 5, :], TAU_LOW, 1.0 / (TAU_HIGH - TAU_LOW), ALU.subtract, ALU.mult))
            gate_step(dve.tensor_scalar(gate[:, 5, :], gate[:, 4, :], 0.0, 1.0, ALU.max, ALU.min))
            gate_step(dve.tensor_scalar(gate[:, 2, :], gate[:, 5, :], scal[:, 1:2], scal[:, 2:3], ALU.mult, ALU.add))
            assert steps[0] == GATE_EXP
            dve.wait_ge(gate_a, 2)
            gate_step(dve.tensor_scalar(gate[:, 4, :], gate[:, 3, :], 1.0, None, ALU.add))
            gate_step(dve.reciprocal(gate[:, 5, :], gate[:, 4, :]))
            gate_step(dve.scalar_tensor_tensor(gate[:, 4, :], gate[:, 5, :], EARLY_EXIT, gate[:, 5, :], ALU.is_ge, ALU.mult))
            gate_step(dve.reciprocal(gate[:, 5, :], wsum_all[:, :]))
            dve.wait_ge(gf_tanh, 1)
            gate_step(dve.scalar_tensor_tensor(gate[:, 10, :], gate[:, 4, :], tanh_gf[:, :], gate[:, 5, :], ALU.mult, ALU.mult))
            gate_step(dve.tensor_scalar(gate[:, 7, :], rstd_all[:, :], tanh_gf[:, :], None, ALU.mult))
            gate_step(dve.tensor_scalar(gate[:, 8, :], gate[:, 7, :], 1.0, None, ALU.add))
            gate_step(dve.scalar_tensor_tensor(gate[:, 9, :], mean_all[:, :], -1.0, gate[:, 7, :], ALU.mult, ALU.mult))
            assert steps[0] == GATE_BASE

            def finish(b, i):
                rows = rows_of(b, i)
                dve.wait_ge(base_done, b * 2 + i + 1)
                dve.wait_ge(aux_summed, b * 2 + i + 1)
                for n in range(4):
                    part = rows[:, 2 * n:2 * n + 2, :]
                    ins = dve.scalar_tensor_tensor(part, psum[0:HALF, 4 * i + n, :].rearrange("p (g c) -> p g c", g=2),
                                                   gate[:, 10, bass.ds(b * 2 + i, 1)], part, ALU.mult, ALU.add)
                ins.then_inc(y_done, 1)

            with dve.Fori(0, BATCH) as b:
                for i in range(2):
                    finish(b, i)


_OUT = (BATCH, SEQ, HID)


def kernel(**inputs):
    import numpy as _np
    import concourse.bacc as _bacc
    from concourse import mybir as _mybir
    from concourse.bass_utils import run_bass_kernel_spmd as _run

    nc = _bacc.Bacc("TRN2", target_bir_lowering=False, num_devices=1)
    a = {k: _np.asarray(v) for k, v in inputs.items()}
    c = a["ctx_1024"]
    laid = {
        "x": a["x"].reshape(BATCH, 2, HALF, PAIRS_A_BATCH, 2, GW).transpose(0, 3, 2, 4, 1, 5).reshape(PAIRS, HALF, 4 * GW),
        "k_t": c.transpose(0, 2, 1).reshape(GROUPS, D, CTX),
        "v_rows": c.reshape(BATCH, NCH, TC, KV, D).transpose(0, 3, 2, 1, 4).reshape(GROUPS, TC, NCH * D),
        "mask": a["mask_SxS2_ff0"].reshape(2, HALF, CTX).transpose(1, 0, 2),
        "g_x": _np.broadcast_to(a["g_xattn"].reshape(1, 1), (HALF, 1)),
        "av_t": a["L0_ffn_aux_values"].T.reshape(KC // 2, 2, 128, NSLOT).transpose(0, 2, 1, 3),
        "wvd_t": a["L0_ffn_Wvd"].T.reshape(KC // 2, 2, 128, VB).transpose(0, 2, 1, 3),
        "w1_t": a["L0_ffn_Wu1"].T.reshape(4, 4, 128, F1).transpose(0, 2, 1, 3),
        "wq_t": a["L0_ffn_Wq"].T.reshape(KC, 128, BOT).transpose(1, 0, 2),
        "wr": a["L0_ffn_Wr"].T,
        "keys_t": a["L0_ffn_aux_keys"].T,
        "log_rel": a["L0_ffn_log_rel"].reshape(1, NSLOT),
        "b1": _np.broadcast_to(a["L0_ffn_bu1"].reshape(1, F1), (HALF, F1)),
        "w2": _np.broadcast_to(a["L0_ffn_Wu2"].reshape(1, F1), (HALF, F1)),
        "wvu_t": a["L0_ffn_Wvu"].T,
        "scalars": _np.broadcast_to(_np.concatenate([a[n].reshape(1) for n in (
            "g_ffn", "L0_ffn_gate_w1", "L0_ffn_gate_bias", "L0_ffn_bu2")]).reshape(1, 4), (HALF, 4)),
    }
    arrays, args = {}, []
    for name, v in laid.items():
        v = _np.ascontiguousarray(v)
        arrays[f"in_{name}"] = v
        args.append(nc.dram_tensor(f"in_{name}", v.shape, _mybir.dt.from_np(v.dtype), kind="ExternalInput").ap())
    o = nc.dram_tensor("out_0", (BATCH, HALF, KV, 2, GW), F32, kind="ExternalOutput").ap()
    flamingo_block(nc, *args, o)
    r = _run(nc, [arrays], core_ids=[0])
    got = r.results[0]["out_0"].reshape(BATCH, HALF, KV, 2, GW).transpose(0, 3, 1, 2, 4).reshape(_OUT)
    return _np.ascontiguousarray(got)
```
